# Optimizing a Trainium2 kernel written in Bass

```python
import numpy as np
import jax
import jax.numpy as jnp

def _softmax(x, axis=-1):
    return jax.nn.softmax(x, axis=axis)

def _gelu(x):
    return jax.nn.gelu(x, approximate=True)

def _silu(x):
    return jax.nn.silu(x)

def _sigmoid(x):
    return jax.nn.sigmoid(x)

def _layernorm(x, axis=-1, eps=1e-05):
    m = jnp.mean(x, axis=axis, keepdims=True)
    v = jnp.var(x, axis=axis, keepdims=True)
    return (x - m) / jnp.sqrt(v + eps)

def _scatter_add(tgt, idx, src, axis=0):
    return tgt.at[idx].add(src)

def _segment_sum(src, seg, n):
    return jax.ops.segment_sum(src, seg, n)
kernel_name = 'mk_seq_preln_d1_jaxref_r4_9fee1b'

def setup_inputs(seed: int=0):
    np.random.seed(seed)
    _w = jnp.asarray

    def _L0_attn_setup():
        import jax, jax.numpy as jnp
        import numpy as np
        from jax import lax
        B, T, HID, NH = (4, 512, 256, 16)
        D = HID // NH
        LN_EPS = 1e-05
        NORM_EPS = 1e-06
        key = jax.random.key(seed)
        ks = jax.random.split(key, 3)
        s = 0.02
        return {'x': jax.random.normal(ks[0], (B, T, HID), jnp.float32), 'ln_g': jnp.ones((HID,), jnp.float32), 'ln_b': jnp.zeros((HID,), jnp.float32), 'w_qkvb': jax.random.normal(ks[1], (HID, 4 * HID), jnp.float32) * s, 'b_qkvb': jnp.zeros((4 * HID,), jnp.float32), 'w_out': jax.random.normal(ks[2], (HID, HID), jnp.float32) * s, 'b_out': jnp.zeros((HID,), jnp.float32)}
    _L0_attn_in = _L0_attn_setup()

    def _L0_ffn_setup():
        import jax, jax.numpy as jnp
        import numpy as np
        B, S, D = (1, 512, 256)
        E, K, F = (64, 8, 192)
        SF = 192
        C = 128
        ROUTED_SCALE = 1.0

        def _moe_forward(x, router_w, w_gate, w_up, w_down, ws_gate_up, ws_down):
            T = x.shape[0]
            logits = x.astype(jnp.float32) @ router_w.T
            probs = jax.nn.softmax(logits, axis=-1)
            topk_w, topk_ids = jax.lax.top_k(probs, K)
            topk_w = topk_w / jnp.sum(topk_w, axis=-1, keepdims=True)
            topk_w = topk_w.astype(x.dtype)
            N = T * K
            flat_e = topk_ids.reshape(-1)
            flat_w = topk_w.reshape(-1)
            tok = jnp.arange(N) // K
            onehot = flat_e[:, None] == jnp.arange(E)[None, :]
            pos = jnp.cumsum(onehot, axis=0)[jnp.arange(N), flat_e] - 1
            valid = pos < C
            idx = jnp.where(valid, flat_e * C + pos, E * C)
            x_buf = jnp.zeros((E * C + 1, x.shape[1]), x.dtype).at[idx].set(x[tok])
            xb = x_buf[:E * C].reshape(E, C, -1)
            g = jnp.einsum('ecd,edf->ecf', xb, w_gate)
            u = jnp.einsum('ecd,edf->ecf', xb, w_up)
            h = jax.nn.silu(g) * u
            y = jnp.einsum('ecf,efd->ecd', h, w_down).reshape(E * C, -1)
            safe = jnp.where(valid, idx, 0)
            contrib = y[safe] * (flat_w * valid.astype(flat_w.dtype))[:, None]
            routed = jax.ops.segment_sum(contrib, tok, num_segments=T)
            routed = routed * ROUTED_SCALE
            gu = x @ ws_gate_up
            sg, su = (gu[:, :SF], gu[:, SF:])
            shared = jax.nn.silu(sg) * su @ ws_down
            return routed + shared
        key = jax.random.key(seed)
        ks = jax.random.split(key, 7)
        w = 0.02
        return {'hidden_states': jax.random.normal(ks[0], (B, S, D), jnp.float32), 'router_w': jax.random.normal(ks[1], (E, D), jnp.float32) * w, 'w_gate': jax.random.normal(ks[2], (E, D, F), jnp.float32) * w, 'w_up': jax.random.normal(ks[3], (E, D, F), jnp.float32) * w, 'w_down': jax.random.normal(ks[4], (E, F, D), jnp.float32) * w, 'ws_gate_up': jax.random.normal(ks[5], (D, 2 * SF), jnp.float32) * w, 'ws_down': jax.random.normal(ks[6], (SF, D), jnp.float32) * w}
    _L0_ffn_in = _L0_ffn_setup()
    _d = {'L0_attn_x': _L0_attn_in['x'], 'L0_attn_ln_g': _L0_attn_in['ln_g'], 'L0_attn_ln_b': _L0_attn_in['ln_b'], 'L0_attn_w_qkvb': _L0_attn_in['w_qkvb'], 'L0_attn_b_qkvb': _L0_attn_in['b_qkvb'], 'L0_attn_w_out': _L0_attn_in['w_out'], 'L0_attn_b_out': _L0_attn_in['b_out'], 'L0_ffn_router_w': _L0_ffn_in['router_w'], 'L0_ffn_w_gate': _L0_ffn_in['w_gate'], 'L0_ffn_w_up': _L0_ffn_in['w_up'], 'L0_ffn_w_down': _L0_ffn_in['w_down'], 'L0_ffn_ws_gate_up': _L0_ffn_in['ws_gate_up'], 'L0_ffn_ws_down': _L0_ffn_in['ws_down']}
    _x0 = _d['L0_attn_x']
    _d['L0_attn_x'] = jax.random.normal(jax.random.fold_in(jax.random.key(seed), 1), (8, 1024, 256), dtype=_x0.dtype)
    del _x0
    return _d

def reference(L0_attn_x, L0_attn_ln_g, L0_attn_ln_b, L0_attn_w_qkvb, L0_attn_b_qkvb, L0_attn_w_out, L0_attn_b_out, L0_ffn_router_w, L0_ffn_w_gate, L0_ffn_w_up, L0_ffn_w_down, L0_ffn_ws_gate_up, L0_ffn_ws_down):

    def _L0_attn_ref(x, ln_g, ln_b, w_qkvb, b_qkvb, w_out, b_out):
        import jax, jax.numpy as jnp
        import numpy as np
        from jax import lax
        B, T, HID, NH = (4, 512, 256, 16)
        D = HID // NH
        LN_EPS = 1e-05
        NORM_EPS = 1e-06
        b, t = x.shape[:2]
        mu = jnp.mean(x, axis=-1, keepdims=True)
        var = jnp.mean((x - mu) ** 2, axis=-1, keepdims=True)
        normed = (x - mu) * lax.rsqrt(var + LN_EPS) * ln_g + ln_b
        proj = normed @ w_qkvb + b_qkvb
        q, k, v, beta_pre = jnp.split(proj, 4, axis=-1)
        beta = jax.nn.sigmoid(beta_pre)

        def heads(a):
            return a.reshape(b, t, NH, D).transpose(1, 0, 2, 3)
        q, k, v, beta = (heads(q), heads(k), heads(v), heads(beta))
        k = k / jnp.maximum(jnp.linalg.norm(k, axis=-1, keepdims=True), NORM_EPS)
        S0 = jnp.zeros((b, NH, D, D), x.dtype)

        def step(S, inp):
            q_t, k_t, v_t, beta_t = inp
            retrieval = jnp.einsum('bhij,bhj->bhi', S, k_t)
            S = S + jnp.einsum('bhi,bhj->bhij', beta_t * (v_t - retrieval), k_t)
            o_t = jnp.einsum('bhij,bhj->bhi', S, q_t)
            return (S, o_t)
        _, out_t = lax.scan(step, S0, (q, k, v, beta))
        scan_out = out_t.transpose(1, 0, 2, 3).reshape(b, t, NH * D)
        return x + scan_out @ w_out + b_out

    def _L0_ffn_ref(hidden_states, router_w, w_gate, w_up, w_down, ws_gate_up, ws_down):
        import jax, jax.numpy as jnp
        import numpy as np
        B, S, D = (1, 512, 256)
        E, K, F = (64, 8, 192)
        SF = 192
        C = 128
        ROUTED_SCALE = 1.0

        def _moe_forward(x, router_w, w_gate, w_up, w_down, ws_gate_up, ws_down):
            T = x.shape[0]
            logits = x.astype(jnp.float32) @ router_w.T
            probs = jax.nn.softmax(logits, axis=-1)
            topk_w, topk_ids = jax.lax.top_k(probs, K)
            topk_w = topk_w / jnp.sum(topk_w, axis=-1, keepdims=True)
            topk_w = topk_w.astype(x.dtype)
            N = T * K
            flat_e = topk_ids.reshape(-1)
            flat_w = topk_w.reshape(-1)
            tok = jnp.arange(N) // K
            onehot = flat_e[:, None] == jnp.arange(E)[None, :]
            pos = jnp.cumsum(onehot, axis=0)[jnp.arange(N), flat_e] - 1
            valid = pos < C
            idx = jnp.where(valid, flat_e * C + pos, E * C)
            x_buf = jnp.zeros((E * C + 1, x.shape[1]), x.dtype).at[idx].set(x[tok])
            xb = x_buf[:E * C].reshape(E, C, -1)
            g = jnp.einsum('ecd,edf->ecf', xb, w_gate)
            u = jnp.einsum('ecd,edf->ecf', xb, w_up)
            h = jax.nn.silu(g) * u
            y = jnp.einsum('ecf,efd->ecd', h, w_down).reshape(E * C, -1)
            safe = jnp.where(valid, idx, 0)
            contrib = y[safe] * (flat_w * valid.astype(flat_w.dtype))[:, None]
            routed = jax.ops.segment_sum(contrib, tok, num_segments=T)
            routed = routed * ROUTED_SCALE
            gu = x @ ws_gate_up
            sg, su = (gu[:, :SF], gu[:, SF:])
            shared = jax.nn.silu(sg) * su @ ws_down
            return routed + shared
        b, s, d = hidden_states.shape
        x = hidden_states.reshape(-1, d)
        out = _moe_forward(x, router_w, w_gate, w_up, w_down, ws_gate_up, ws_down)
        return out.reshape(b, s, d)
    x = L0_attn_x
    x = x + _L0_attn_ref(_layernorm(x, axis=-1), L0_attn_ln_g, L0_attn_ln_b, L0_attn_w_qkvb, L0_attn_b_qkvb, L0_attn_w_out, L0_attn_b_out)
    x = x + _L0_ffn_ref(_layernorm(x, axis=-1), L0_ffn_router_w, L0_ffn_w_gate, L0_ffn_w_up, L0_ffn_w_down, L0_ffn_ws_gate_up, L0_ffn_ws_down)
    return x

_drawn_inputs = setup_inputs


def setup_inputs(seed=0):
    import zlib

    import numpy as np

    out = dict(_drawn_inputs(seed))
    spreads = {'L0_attn_ln_g': (1.0, 0.6),
     'L0_attn_ln_b': (0.0, 0.8),
     'L0_attn_b_qkvb': (0.0, 0.318),
     'L0_attn_b_out': (0.0, 0.1)}
    factors = {'L0_ffn_router_w': 8.0,
     'L0_ffn_w_gate': 8.0,
     'L0_ffn_w_up': 8.0,
     'L0_ffn_w_down': 8.0,
     'L0_ffn_ws_gate_up': 7.707,
     'L0_ffn_ws_down': 7.739}
    for name, (base, spread) in spreads.items():
        noise = np.random.default_rng([zlib.crc32(name.encode()), seed]).standard_normal(out[name].shape)
        drawn = base * np.exp(spread * noise) if base else spread * noise
        out[name] = jnp.asarray(drawn.astype(out[name].dtype))
    for name, factor in factors.items():
        out[name] = (out[name] * factor).astype(out[name].dtype)
    return out
```

```python
import concourse.bass as bass
from concourse import mybir
from contextlib import ExitStack

F32 = mybir.dt.float32
BF16 = mybir.dt.bfloat16
U32 = mybir.dt.uint32
ALU = mybir.AluOpType
ACT = mybir.ActivationFunctionType
AX = mybir.AxisListType

B, T, D = 8, 1024, 256
NH, HD = 16, 16
NT = B * T
P = 128
TILES = NT // P
BT = T // P
KC = D // P
GT = 4
GN = GT * P
GROUPS = TILES // GT
PROJ = 4 * D
PC = PROJ // P
E, TOPK, CAP, F = 64, 8, 128, 192
FH = F // 2
ROW = D + E
EPS, NORM_EPS = 1e-5, 1e-6
WIN = 128
NWIN = T // WIN
U = 16
HU = U // 2


class Chain:

    def __init__(self, eng, sem, base=0, first=1):
        self.eng, self.sem, self.base, self.first, self.n = eng, sem, base, first, 0

    def __call__(self, ins):
        ins.then_inc(self.sem, 1)
        self.n += 1
        self.eng.wait_ge(self.sem, self.base + self.n + self.first)


def mid(ap, count):
    return ap.rearrange("p (o n) -> p o n", o=1).broadcast_to([ap.shape[0], count, ap.shape[1]])


def prime(nc, sems):
    with nc.Block() as block:
        @block.sync
        def _(sp):
            for s in sems:
                sp.nop().then_inc(s, 1)


def build(nc, x, ln_g, ln_b, w_qkvb, b_qkvb, w_out, b_out, router_w, w_gate, w_up, w_down, ws_gate_up,
          ws_down, out):
    scratch = [nc.dram_tensor(n, s, F32, kind="Internal").ap() for n, s in (
        ("lanes_dram", (B, PROJ, T)), ("scan_dram", (B, D, T)), ("rows_dram", (NT + P, ROW)),
        ("counts_dram", (E * TILES, P)), ("ends_dram", (1, E * TILES)))]
    lanes_dram, scan_dram, rows_dram, counts_dram, ends_dram = scratch
    with ExitStack() as keep:
        def sb(name, shape, dt=F32):
            return keep.enter_context(nc.sbuf_tensor(name, shape, dt))

        m = {
            "x": sb("x_sb", [P, TILES, D]),
            "ident": sb("ident", [P, P]),
            "mu": sb("mu", [P, TILES]), "var": sb("var", [P, TILES]),
            "stats": sb("stats", [P, TILES, 6]),
            "r1": sb("r1", [P, TILES]), "r12": sb("r12", [P, TILES]), "shift": sb("shift", [P, TILES]),
            "rs1": sb("rs1", [P, TILES]), "shift1": sb("shift1", [P, TILES]),
            "tmp": sb("tmp", [P, TILES]), "tmp2": sb("tmp2", [P, TILES]),
        }
        moments(nc, m, x)
        project(nc, m, ln_g, ln_b, w_qkvb, b_qkvb, lanes_dram)
        scan(nc, m, lanes_dram, scan_dram)
        attn_out(nc, m, scan_dram, w_out, b_out)
        route(nc, m, router_w, ws_gate_up, ws_down, rows_dram, counts_dram, ends_dram, out)
    experts(nc, w_gate, w_up, w_down, rows_dram, counts_dram, ends_dram, out)


def row_moments(v, link, m):
    half = lambda i: m["stats"][:, :, i]
    link(v.tensor_tensor(m["mu"][:], half(1), half(4), ALU.add))
    link(v.tensor_tensor(m["tmp"][:], half(1), half(4), ALU.subtract))
    link(v.tensor_scalar(m["mu"][:], m["mu"][:], 0.5, None, ALU.mult))
    link(v.tensor_scalar(m["tmp"][:], m["tmp"][:], 0.5, None, ALU.mult))
    link(v.tensor_tensor(m["tmp"][:], m["tmp"][:], m["tmp"][:], ALU.mult))
    link(v.tensor_tensor(m["var"][:], half(2), half(5), ALU.add))
    link(v.scalar_tensor_tensor(m["var"][:], m["var"][:], 1.0 / D, m["tmp"][:], ALU.mult, ALU.add))


def moments(nc, m, x):
    with ExitStack() as c:
        x_in, stat, chain, need_sqrt, have_sqrt, id0 = (
            c.enter_context(nc.semaphore("mo_" + n)) for n in ("x_in", "stat", "chain", "need_sqrt", "have_sqrt", "id0"))
        eps = c.enter_context(nc.sbuf_tensor("mo_eps", [P, 1], F32))
        block = c.enter_context(nc.Block())

        @block.sync
        def _(sp):
            for b in range(B):
                sp.dma_start(m["x"][:, b * BT:(b + 1) * BT, :],
                             x[b].rearrange("(n p) d -> p n d", p=P)).then_inc(x_in, 16)

        @block.gpsimd
        def _(pool):
            pool.memset(m["ident"][:], 0.0).then_inc(id0, 1)
            pool.wait_ge(id0, 1)
            pool.affine_select(out=m["ident"][:], in_=m["ident"][:], compare_op=ALU.not_equal, fill=1.0,
                               base=0, pattern=[[-1, P]], channel_multiplier=1).then_inc(id0, 1)

        @block.scalar
        def _(act):
            act.wait_ge(need_sqrt, 1)
            act.activation(m["r1"][:], m["var"][:], ACT.Sqrt, bias=eps[:]).then_inc(have_sqrt, 1)
            act.wait_ge(need_sqrt, 2)
            act.activation(m["r12"][:], m["tmp"][:], ACT.Sqrt, bias=eps[:]).then_inc(have_sqrt, 1)

        @block.vector
        def _(v):
            link = Chain(v, chain, first=0)
            link(v.memset(eps[:], EPS))
            v.wait_ge(x_in, 16 * B)
            with v.Fori(0, B) as b:
                for r in range(BT):
                    n = b * BT + r
                    v.bn_stats(m["stats"][:, bass.ds(n, 1), :].rearrange("p o s -> p (o s)"),
                               m["x"][:, bass.ds(n, 1), :].rearrange("p o d -> p (o d)")).then_inc(stat, 1)
            v.wait_ge(stat, TILES)
            row_moments(v, link, m)
            v.nop().then_inc(need_sqrt, 1)
            v.wait_ge(have_sqrt, 1)
            link(v.reciprocal(m["r1"][:], m["r1"][:]))
            link(v.tensor_tensor(m["tmp"][:], m["var"][:], m["r1"][:], ALU.mult))
            link(v.tensor_tensor(m["tmp"][:], m["tmp"][:], m["r1"][:], ALU.mult))
            v.nop().then_inc(need_sqrt, 1)
            v.wait_ge(have_sqrt, 2)
            link(v.reciprocal(m["r12"][:], m["r12"][:]))
            link(v.tensor_tensor(m["r12"][:], m["r12"][:], m["r1"][:], ALU.mult))
            link(v.scalar_tensor_tensor(m["shift"][:], m["mu"][:], -1.0, m["r12"][:], ALU.mult, ALU.mult))
            link(v.scalar_tensor_tensor(m["shift1"][:], m["mu"][:], -1.0, m["r1"][:], ALU.mult, ALU.mult))
            link(v.tensor_scalar(m["rs1"][:], m["r1"][:], 1.0, None, ALU.add))


def project(nc, m, ln_g, ln_b, w_qkvb, b_qkvb, lanes_dram):
    with ExitStack() as c:
        def sb(name, shape, dt=F32):
            return c.enter_context(nc.sbuf_tensor("pj_" + name, shape, dt))

        sems = []

        def sem(name):
            sems.append(c.enter_context(nc.semaphore("pj_" + name)))
            return sems[-1]

        W = sb("w_qkvb_sb", [P, KC, PROJ])
        bias, gain, off = sb("bias", [P, PC]), sb("gain", [P, KC]), sb("off", [P, KC])
        xh, nT, stage = sb("xh", [P, GT, D]), sb("nT", [P, 2, KC, GN]), sb("stage", [P, 2, PC, GN])
        tp = [c.enter_context(nc.psum_tensor(f"pj_tp{k}", [P, GN], F32)) for k in range(KC)]
        pj = [c.enter_context(nc.psum_tensor(f"pj_pj{k}", [P, GN], F32)) for k in range(4)]
        w_in, xh_ready, tp_ready, nT_ready, pj_ready, dve_out, act_out = map(sem, (
            "w_in", "xh_ready", "tp_ready", "nT_ready", "pj_ready", "dve_out", "act_out"))
        stored = [sem("stored0"), sem("stored1")]
        LOADS = 4 * (KC + 2) + 2
        prime(nc, sems)
        block = c.enter_context(nc.Block())

        @block.sync
        def _(sp):
            for a in range(4):
                for k in range(KC):
                    sp.dma_start(W[:, k, :].rearrange("p (h a j) -> p h a j", a=4, j=HD)[:, :, a, :],
                                 w_qkvb[k * P:(k + 1) * P, a * D:(a + 1) * D].rearrange("p (h j) -> p h j", j=HD)
                                 ).then_inc(w_in, 16)
                for h in range(2):
                    row = h * 4 * HD + a * HD
                    sp.dma_start(bias[row:row + HD, :],
                                 b_qkvb[a * D:(a + 1) * D].rearrange("(c h j) -> h j c", h=2, j=HD)[h],
                                 allow_slow_non_contiguous=True).then_inc(w_in, 16)
            sp.dma_start(gain[:], ln_g.rearrange("(c p) -> p c", p=P), allow_slow_non_contiguous=True).then_inc(w_in, 16)
            sp.dma_start(off[:], ln_b.rearrange("(c p) -> p c", p=P), allow_slow_non_contiguous=True).then_inc(w_in, 16)
            with sp.Fori(0, B) as b:
                for s in range(2):
                    sp.wait_ge(dve_out, b * 8 + 4 * (s + 1) + 1)
                    sp.wait_ge(act_out, b * 8 + 4 * (s + 1) + 1)
                    sp.dma_start(lanes_dram[bass.ds(b, 1), :, s * GN:(s + 1) * GN].rearrange("o (c p) t -> p (o c) t", p=P),
                                 stage[:, s]).then_inc(stored[s], 16)
            sp.wait_ge(stored[0], 16 * B + 1)
            sp.wait_ge(stored[1], 16 * B + 1)

        @block.vector
        def _(v):
            v.wait_ge(w_in, 16 * LOADS + 1)
            with v.Fori(0, B) as b:
                for s in range(2):
                    v.wait_ge(tp_ready, b * 2 + s + 1)
                    for r in range(GT):
                        n = b * BT + (s * GT + r)
                        v.tensor_scalar(xh[:, r, :], m["x"][:, bass.ds(n, 1), :].rearrange("p o d -> p (o d)"),
                                        m["r12"][:, bass.ds(n, 1)], m["shift"][:, bass.ds(n, 1)],
                                        ALU.mult, ALU.add).then_inc(xh_ready, 1)
                    v.wait_ge(stored[s], b * 16 + 1)
                    for k in range(4):
                        v.wait_ge(pj_ready, b * 16 + (8 * s + k + 1) + 1)
                        v.tensor_scalar(stage[:, s, k, :], pj[k][:], bias[:, k:k + 1], None,
                                        ALU.add).then_inc(dve_out, 1)

        @block.scalar
        def _(act):
            act.wait_ge(w_in, 16 * LOADS + 1)
            with act.Fori(0, B) as b:
                for s in range(2):
                    act.wait_ge(tp_ready, b * 2 + (s + 1) + 1)
                    act.wait_ge(pj_ready, b * 16 + 8 * s + 1)
                    for k in range(KC):
                        act.activation(nT[:, s, k, :], tp[k][:], ACT.Identity, bias=off[:, k:k + 1],
                                       scale=gain[:, k:k + 1]).then_inc(nT_ready, 1)
                    act.wait_ge(stored[s], b * 16 + 1)
                    for k in range(4, PC):
                        act.wait_ge(pj_ready, b * 16 + (8 * s + k + 1) + 1)
                        act.activation(stage[:, s, k, :], pj[k % 4][:], ACT.Identity,
                                       bias=bias[:, k:k + 1]).then_inc(act_out, 1)

        @block.tensor
        def _(pe):
            with pe.Fori(0, B) as b:
                for s in range(2):
                    pe.wait_ge(nT_ready, b * 4 + 2 * s + 1)
                    pe.wait_ge(xh_ready, b * 8 + 4 * (s + 1) + 1)
                    for r in range(GT):
                        for k in range(KC):
                            last = pe.transpose(tp[k][:, r * P:(r + 1) * P], xh[:, r, k * P:(k + 1) * P],
                                                m["ident"][:])
                    last.then_inc(tp_ready, 1)
                    pe.wait_ge(nT_ready, b * 4 + 2 * (s + 1) + 1)
                    for k in range(PC):
                        if k < 4:
                            pe.wait_ge(act_out, b * 8 + 4 * s + 1)
                        else:
                            pe.wait_ge(dve_out, b * 8 + (4 * s + k - 3) + 1)
                        for j in range(KC):
                            last = pe.matmul(pj[k % 4][:], W[:, j, k * P:(k + 1) * P], nT[:, s, j, :],
                                             start=j == 0, stop=j == KC - 1)
                        last.then_inc(pj_ready, 1)


def scan(nc, m, lanes_dram, scan_dram):
    with ExitStack() as c:
        def sb(name, shape, dt=F32):
            return c.enter_context(nc.sbuf_tensor("sc_" + name, shape, dt))

        sems = []

        def sem(name):
            sems.append(c.enter_context(nc.semaphore("sc_" + name)))
            return sems[-1]

        lanes = sb("lanes", [P, 2, 4, HD, WIN])
        S = sb("S", [P, U, HD, HD])
        prod, outer = sb("prod", [P, HD, HD]), sb("outer", [P, HD, HD])
        ret, diff, u = sb("ret", [P, HD]), sb("diff", [P, HD]), sb("u", [P, HD])
        SQ = sb("SQ", [P, 2, HU, HD * HD])
        sq, norm = sb("sq", [P, HD, WIN]), sb("norm", [P, WIN])
        ow = sb("ow", [P, 2, HD, WIN])
        carrier = sb("carrier", [P, 3])
        red = [c.enter_context(nc.psum_tensor(f"sc_red{k}", [P, 512], F32)) for k in range(2)]
        step, sq_ready, ss_ready, norm_ready, prep, SQ_ready, SQ_used, ow_ready, beta_ready, carrier_set = map(sem, (
            "step", "sq_ready", "ss_ready", "norm_ready", "prep", "SQ_ready", "SQ_used", "ow_ready", "beta_ready",
            "carrier_set"))
        loaded, stored = [sem("loaded0"), sem("loaded1")], [sem("out0"), sem("out1")]
        prime(nc, sems)
        block = c.enter_context(nc.Block())
        q_, k_, v_, b_ = range(4)
        OPS = 6

        def load(sp, w, s):
            sp.dma_start(lanes[:, s].rearrange("p a j t -> p (a j) t"),
                         lanes_dram.rearrange("b (h r) t -> (b h) r t", h=NH)[:, :, bass.ds(w * WIN, WIN)]
                         ).then_inc(loaded[s], 16)

        def store(sp, w, s):
            sp.wait_ge(ow_ready, w * 16 + 16 + 1)
            sp.dma_start(scan_dram.rearrange("b (h i) t -> (b h) i t", i=HD)[:, :, bass.ds(w * WIN, WIN)],
                         ow[:, s]).then_inc(stored[s], 16)

        @block.sync
        def _(sp):
            load(sp, 0, 0)
            load(sp, 1, 1)
            with sp.Fori(0, NWIN // 2 - 1) as p:
                for s in range(2):
                    w = p * 2 + s
                    sp.wait_ge(step, w * (WIN * OPS) + (WIN * OPS + 1) + 1)
                    sp.wait_ge(SQ_ready, w * 16 + (16 + 2) + 1)
                    load(sp, w + 2, s)
                    store(sp, w, s)
            for s in range(2):
                store(sp, NWIN - 2 + s, s)
            for s in range(2):
                sp.wait_ge(stored[s], 16 * (NWIN // 2) + 1)

        @block.scalar
        def _(act):
            with act.Fori(0, NWIN // 2) as p:
                for s in range(2):
                    w = p * 2 + s
                    act.wait_ge(loaded[s], p * 16 + 16 + 1)
                    act.wait_ge(ss_ready, w + 1)
                    act.activation(lanes[:, s, b_], lanes[:, s, b_], ACT.Sigmoid).then_inc(beta_ready, 1)
                    act.activation(sq[:], lanes[:, s, k_], ACT.Square).then_inc(sq_ready, 1)
                    act.wait_ge(ss_ready, w + 1 + 1)
                    act.activation(norm[:], norm[:], ACT.Sqrt).then_inc(norm_ready, 1)
                    act.wait_ge(stored[s], p * 16 + 1)
                    with act.Fori(0, WIN // U) as it:
                        for h in range(2):
                            act.wait_ge(SQ_used, w * 16 + it * 2 + (h + 1) + 1)
                            act.activation(ow[:, s, :, bass.ds(it * U + h * HU, HU)].rearrange("p i t -> p t i"),
                                           red[h][:, 0:HU * HD].rearrange("p (t i) -> p t i", i=HD), ACT.Copy
                                           ).then_inc(ow_ready, 1)

        @block.tensor
        def _(pe):
            with pe.Fori(0, T // U) as it:
                for h in range(2):
                    pe.wait_ge(SQ_ready, it * 2 + (h + 3) + 1)
                    pe.wait_ge(ow_ready, it * 2 + 1)
                    for j in range(HD):
                        last = pe.matmul(red[h][:, 0:HU * HD], m["ident"][:],
                                         SQ[:, h].rearrange("p t (i j) -> p (t i) j", j=HD)[:, :, j],
                                         start=j == 0, stop=j == HD - 1)
                    last.then_inc(SQ_used, 1)

        @block.gpsimd
        def _(pool):
            pool.memset(carrier[:, 2:3], 0.0).then_inc(carrier_set, 1)
            pool.wait_ge(carrier_set, 2)
            pool.memset(SQ[:], 0.0).then_inc(SQ_ready, 2)
            pool.wait_ge(SQ_ready, 3)
            with pool.Fori(0, NWIN // 2) as p:
                for s in range(2):
                    w = p * 2 + s
                    pool.wait_ge(loaded[s], p * 16 + 16 + 1)
                    pool.tensor_tensor(carrier[:, 1:2], carrier[:, 2:3], carrier[:, 2:3], ALU.add)
                    with pool.Fori(0, WIN // U) as it:
                        for h in range(2):
                            pool.wait_ge(step, w * (WIN * OPS) + it * (U * OPS) + (1 + HU * OPS * (h + 1)) + 1)
                            pool.wait_ge(SQ_used, w * 16 + it * 2 + 1)
                            for i in range(HU):
                                last = pool.tensor_tensor(
                                    SQ[:, h, i].rearrange("p (i j) -> p i j", j=HD), S[:, h * HU + i],
                                    lanes[:, s, q_, :, bass.ds(it * U + (h * HU + i), 1)].rearrange("p j o -> p o j")
                                    .broadcast_to([P, HD, HD]), ALU.mult)
                            last.then_inc(SQ_ready, 1)

        @block.vector
        def _(v):
            v.memset(S[:, U - 1], 0.0).then_inc(step, 1)
            with v.Fori(0, NWIN // 2) as p:
                for s in range(2):
                    w = p * 2 + s
                    K = lanes[:, s, k_]
                    v.wait_ge(sq_ready, w + 1 + 1)
                    v.tensor_reduce(norm[:], sq[:].rearrange("p j t -> p t j"), AX.X, ALU.add).then_inc(ss_ready, 1)
                    v.wait_ge(norm_ready, w + 1 + 1)
                    v.tensor_scalar(norm[:], norm[:], NORM_EPS, None, ALU.max).then_inc(prep, 1)
                    v.wait_ge(prep, w * 3 + 1 + 1)
                    v.reciprocal(norm[:], norm[:]).then_inc(prep, 1)
                    v.wait_ge(prep, w * 3 + 2 + 1)
                    v.tensor_tensor(K, K, mid(norm[:], HD), ALU.mult).then_inc(prep, 1)
                    v.wait_ge(prep, w * 3 + 3 + 1)
                    v.wait_ge(beta_ready, w + 1 + 1)
                    v.memset(carrier[:, 0:1], 0.0)
                    with v.Fori(0, WIN // U) as it:
                        for i in range(U):
                            n = w * (WIN * OPS) + it * (U * OPS) + (i * OPS + 1)
                            at = bass.ds(it * U + i, 1)
                            key = lanes[:, s, k_, :, at].rearrange("p j o -> p o j").broadcast_to([P, HD, HD])
                            old, new = S[:, (i - 1) % U], S[:, i]
                            v.wait_ge(step, n + 1)
                            v.tensor_tensor(prod[:], old, key, ALU.mult).then_inc(step, 1)
                            v.wait_ge(step, n + 1 + 1)
                            v.tensor_reduce(ret[:], prod[:], AX.X, ALU.add).then_inc(step, 1)
                            v.wait_ge(step, n + 2 + 1)
                            v.tensor_tensor(diff[:], lanes[:, s, v_, :, at].rearrange("p i o -> p (i o)"), ret[:],
                                            ALU.subtract).then_inc(step, 1)
                            v.wait_ge(step, n + 3 + 1)
                            v.tensor_tensor(u[:], lanes[:, s, b_, :, at].rearrange("p i o -> p (i o)"), diff[:],
                                            ALU.mult).then_inc(step, 1)
                            v.wait_ge(step, n + 4 + 1)
                            v.tensor_tensor(outer[:], u[:].rearrange("p (i o) -> p i o", o=1).broadcast_to([P, HD, HD]),
                                            key, ALU.mult).then_inc(step, 1)
                            v.wait_ge(step, n + 5 + 1)
                            if i % HU == 0:
                                v.wait_ge(SQ_ready, w * 16 + it * 2 + (1 + i // HU) + 1)
                            v.tensor_tensor(new, old, outer[:], ALU.add).then_inc(step, 1)


def attn_out(nc, m, scan_dram, w_out, b_out):
    with ExitStack() as c:
        def sb(name, shape, dt=F32):
            return c.enter_context(nc.sbuf_tensor("ao_" + name, shape, dt))

        sems = []

        def sem(name):
            sems.append(c.enter_context(nc.semaphore("ao_" + name)))
            return sems[-1]

        W, brow, ones = sb("w_out_sb", [P, KC, D]), sb("brow", [1, D]), sb("ones", [1, P])
        oT, eps = sb("oT", [P, 2, KC, GN]), sb("eps", [P, 1])
        ps = [c.enter_context(nc.psum_tensor(f"ao_ps{k}", [P, 512], F32)) for k in range(4)]
        w_in, x_scaled, y_ready, stat, chain, need_sqrt, have_sqrt, consts = map(sem, (
            "w_in", "x_scaled", "y_ready", "stat", "chain", "need_sqrt", "have_sqrt", "consts"))
        o_in = [sem("o_in0"), sem("o_in1")]
        prime(nc, sems)
        block = c.enter_context(nc.Block())

        @block.sync
        def _(sp):
            sp.dma_start(W[:], w_out.rearrange("(k p) f -> p k f", p=P)).then_inc(w_in, 16)
            sp.dma_start(brow[:], b_out.rearrange("(o f) -> o f", o=1)).then_inc(w_in, 16)
            with sp.Fori(0, B) as b:
                for s in range(2):
                    sp.wait_ge(y_ready, b * 8 + 1)
                    sp.dma_start(oT[:, s], scan_dram[bass.ds(b, 1), :, s * GN:(s + 1) * GN]
                                 .rearrange("o (c p) t -> p (o c) t", p=P)).then_inc(o_in[s], 16)

        @block.tensor
        def _(pe):
            pe.wait_ge(w_in, 33)
            pe.wait_ge(consts, 3)
            with pe.Fori(0, B) as b:
                for s in range(2):
                    pe.wait_ge(o_in[s], b * 16 + 16 + 1)
                    for r in range(GT):
                        pe.wait_ge(stat, b * 8 + 4 * s + 1)
                        pe.matmul(ps[r][:, 0:D], ones[:], brow[:], start=True, stop=False)
                        for k in range(KC):
                            last = pe.matmul(ps[r][:, 0:D], oT[:, s, k, r * P:(r + 1) * P], W[:, k, :],
                                             start=False, stop=k == KC - 1)
                        last.then_inc(y_ready, 1)

        @block.scalar
        def _(act):
            with act.Fori(0, B) as b:
                for r in range(BT):
                    n = b * BT + r
                    xt = m["x"][:, bass.ds(n, 1), :].rearrange("p o d -> p (o d)")
                    act.activation(xt, xt, ACT.Identity, bias=m["shift1"][:, bass.ds(n, 1)],
                                   scale=m["rs1"][:, bass.ds(n, 1)]).then_inc(x_scaled, 1)
            act.wait_ge(need_sqrt, 2)
            act.activation(m["r1"][:], m["var"][:], ACT.Sqrt, bias=eps[:]).then_inc(have_sqrt, 1)

        @block.vector
        def _(v):
            link = Chain(v, chain)
            v.memset(ones[:], 1.0).then_inc(consts, 1)
            v.memset(eps[:], EPS).then_inc(consts, 1)
            with v.Fori(0, B) as b:
                for r in range(BT):
                    n = b * BT + r
                    xt = m["x"][:, bass.ds(n, 1), :].rearrange("p o d -> p (o d)")
                    v.wait_ge(x_scaled, n + 1 + 1)
                    v.wait_ge(y_ready, n + 1 + 1)
                    v.tensor_tensor(xt, xt, ps[r % GT][:, 0:D], ALU.add).then_inc(chain, 1)
                    v.wait_ge(chain, n + 1 + 1)
                    v.bn_stats(m["stats"][:, bass.ds(n, 1), :].rearrange("p o s -> p (o s)"), xt).then_inc(stat, 1)
            v.wait_ge(stat, TILES + 1)
            link.base = TILES
            row_moments(v, link, m)
            v.nop().then_inc(need_sqrt, 1)
            v.wait_ge(have_sqrt, 2)
            link(v.reciprocal(m["r1"][:], m["r1"][:]))
            link(v.scalar_tensor_tensor(m["shift1"][:], m["mu"][:], -1.0, m["r1"][:], ALU.mult, ALU.mult))


def route(nc, m, router_w, ws_gate_up, ws_down, rows_dram, counts_dram, ends_dram, out):
    with ExitStack() as c:
        def sb(name, shape, dt=F32):
            return c.enter_context(nc.sbuf_tensor("rt_" + name, shape, dt))

        sems = []

        def sem(name):
            sems.append(c.enter_context(nc.semaphore("rt_" + name)))
            return sems[-1]

        RW, RT = sb("router_rows", [E, D]), sb("router_T", [P, KC, E])
        GU, DN = sb("shared_gu", [P, KC, 2 * F]), sb("shared_dn", [FH, 2, D])
        rows, hT = sb("rows", [P, 2, GT, ROW]), sb("hT", [P, 2, KC, GN])
        neg, m8, e8 = sb("neg", [P, GT]), sb("m8", [P, GT, TOPK]), sb("e8", [P, GT, TOPK])
        ex, rep, mask = sb("ex", [P, GT, E]), sb("rep", [P, GT, E]), sb("mask", [P, GT, E], BF16)
        tri, trif = sb("tri", [P, P + 1], BF16), sb("trif", [P, P + 1])
        cnt, tot = sb("cnt", [E, 2, GT, P]), sb("tot", [E, TILES])
        wsum, carrier = sb("wsum", [P, GT]), sb("carrier", [P, 1])
        th, act_in = sb("th", [FH, 2, GN]), sb("act_in", [FH, 2, GN])
        zero, onesE = sb("zero", [P, ROW]), sb("onesE", [E, TILES])
        tp = [c.enter_context(nc.psum_tensor(f"rt_tp{k}", [P, GN], F32)) for k in range(KC)]
        lg = c.enter_context(nc.psum_tensor("rt_lg", [P, GT, P], F32))
        cp = c.enter_context(nc.psum_tensor("rt_cp", [E, 2, 512], F32))
        gu = [c.enter_context(nc.psum_tensor(f"rt_gu{k}", [P, GN], F32)) for k in range(3)]
        names = ("w_in consts h_ready tp_ready hT_ready lg_ready mx ex_ready topk mask_ready cp_ready cnt_ready "
                 "gate_ready up_ready th_ready t_done a_done dn_ready x_done chain tail_sem id0 rt0 group_chain").split()
        q = {n: sem(n) for n in names}
        rows_out, cnt_out, base_out = ([sem(f"{n}{s}") for s in range(2)] for n in ("rows_out", "cnt_out", "base_out"))
        prime(nc, sems)
        block = c.enter_context(nc.Block())
        groups = 2 * B

        @block.sync
        def _(sp):
            sp.dma_start(RW[:], router_w).then_inc(q["w_in"], 16)
            sp.dma_start(GU[:], ws_gate_up.rearrange("(k p) f -> p k f", p=P)).then_inc(q["w_in"], 16)
            sp.dma_start(DN[:], ws_down.rearrange("(k p) f -> p k f", p=FH)).then_inc(q["w_in"], 16)
            sp.wait_ge(q["consts"], 2)
            sp.dma_start(rows_dram[NT:NT + P, :], zero[:]).then_inc(q["tail_sem"], 16)
            sp.dma_start(out[NT:NT + P, :], zero[:, 0:D]).then_inc(q["tail_sem"], 16)
            with sp.Fori(0, B) as b:
                for s in range(2):
                    g = b * 2 + s
                    sp.wait_ge(q["mask_ready"], g + 1 + 1)
                    sp.dma_start(rows_dram.rearrange("(n p) f -> p n f", p=P)[:, bass.ds(g * GT, GT), :],
                                 rows[:, s]).then_inc(rows_out[s], 16)
                    sp.wait_ge(q["cnt_ready"], g + 1 + 1)
                    sp.dma_start(counts_dram.rearrange("(e n) t -> e n t", e=E)[:, bass.ds(g * GT, GT), :],
                                 cnt[:, s]).then_inc(cnt_out[s], 16)
                    sp.wait_ge(q["x_done"], g * GT + GT + 1)
                    sp.dma_start(out.rearrange("(n p) f -> p n f", p=P)[:, bass.ds(g * GT, GT), :],
                                 m["x"][:, bass.ds(g * GT, GT), :]).then_inc(base_out[s], 16)
            sp.wait_ge(q["chain"], 2)
            sp.dma_start(ends_dram.rearrange("o (e n) -> (o e) n", e=E), tot[:]).then_inc(q["tail_sem"], 16)
            sp.wait_ge(q["tail_sem"], 49)
            for s in range(2):
                for x in (rows_out, cnt_out, base_out):
                    sp.wait_ge(x[s], 16 * B + 1)

        @block.gpsimd
        def _(pool):
            pool.memset(zero[:], 0.0).then_inc(q["consts"], 1)
            pool.memset(onesE[:], 1.0).then_inc(q["consts"], 1)
            pool.memset(trif[:], 2.0).then_inc(q["id0"], 1)
            pool.wait_ge(q["id0"], 2)
            pool.affine_select(out=trif[:, 0:P], in_=trif[:, 0:P], compare_op=ALU.is_ge, fill=0.0, base=0,
                               pattern=[[1, P]], channel_multiplier=-1).then_inc(q["id0"], 1)
            pool.wait_ge(q["id0"], 3)
            pool.tensor_tensor(trif[:, 0:P], trif[:, 0:P], m["ident"][:], ALU.subtract).then_inc(q["id0"], 1)
            pool.wait_ge(q["id0"], 4)
            pool.tensor_copy(tri[:], trif[:]).then_inc(q["consts"], 1)

        @block.tensor
        def _(pe):
            pe.wait_ge(q["w_in"], 49)
            for k in range(KC):
                last = pe.transpose(tp[k][:, 0:E], RW[:, k * P:(k + 1) * P], m["ident"][0:E, 0:E])
            last.then_inc(q["rt0"], 1)
            pe.wait_ge(q["rt0"], 4)
            pe.wait_ge(q["consts"], 4)
            with pe.Fori(0, B) as b:
                for s in range(2):
                    g = b * 2 + s
                    pe.wait_ge(q["hT_ready"], g * 2 + 1)
                    pe.wait_ge(q["h_ready"], g * GT + GT + 1)
                    for r in range(GT):
                        for k in range(KC):
                            last = pe.transpose(tp[k][:, r * P:(r + 1) * P], rows[:, s, r, k * P:(k + 1) * P],
                                                m["ident"][:])
                    last.then_inc(q["tp_ready"], 1)
                    pe.wait_ge(q["hT_ready"], g * 2 + 2 + 1)
                    pe.wait_ge(q["ex_ready"], g * GT + 1)
                    for r in range(GT):
                        for k in range(KC):
                            last = pe.matmul(lg[:, r, 0:E], hT[:, s, k, r * P:(r + 1) * P], RT[:, k, :],
                                             start=k == 0, stop=k == KC - 1)
                    last.then_inc(q["lg_ready"], 1)
                    for f in range(2):
                        pe.wait_ge(q["t_done"], g * 2 + f + 1)
                        for j in range(KC):
                            last = pe.matmul(gu[0][0:FH, :], GU[:, j, f * FH:(f + 1) * FH], hT[:, s, j, :],
                                             start=j == 0, stop=j == KC - 1)
                        last.then_inc(q["gate_ready"], 1)
                        pe.wait_ge(q["a_done"], g * 2 + f + 1)
                        for j in range(KC):
                            last = pe.matmul(gu[1][0:FH, :], GU[:, j, F + f * FH:F + (f + 1) * FH], hT[:, s, j, :],
                                             start=j == 0, stop=j == KC - 1)
                        last.then_inc(q["up_ready"], 1)
                    pe.wait_ge(q["mask_ready"], g + 1 + 1)
                    pe.wait_ge(q["cnt_ready"], g + 1)
                    for r in range(GT):
                        last = pe.matmul(cp[:, r // 2, (r % 2) * 256:(r % 2) * 256 + P + 1], mask[:, r, :], tri[:],
                                         start=True, stop=True)
                    last.then_inc(q["cp_ready"], 1)
                    pe.wait_ge(q["a_done"], g * 2 + 2 + 1)
                    for r in range(GT):
                        h = r % 2
                        pe.wait_ge(q["x_done"], g * GT + r + 1)
                        for f in range(2):
                            last = pe.matmul(gu[2][:, 0:D], act_in[:, f, r * P:(r + 1) * P], DN[:, f, :],
                                             start=f == 0, stop=f == 1)
                        last.then_inc(q["dn_ready"], 1)

        @block.scalar
        def _(act):
            act.wait_ge(q["rt0"], 2)
            for k in range(KC):
                act.copy(RT[:, k, :], tp[k][:, 0:E]).then_inc(q["rt0"], 1)
            with act.Fori(0, B) as b:
                for s in range(2):
                    g = b * 2 + s
                    act.wait_ge(rows_out[s], b * 16 + 1)
                    for r in range(GT):
                        n = b * BT + (s * GT + r)
                        act.activation(rows[:, s, r, 0:D], m["x"][:, bass.ds(n, 1), :].rearrange("p o d -> p (o d)"),
                                       ACT.Identity, bias=m["shift1"][:, bass.ds(n, 1)], scale=m["r1"][:, bass.ds(n, 1)]
                                       ).then_inc(q["h_ready"], 1)
                    act.wait_ge(q["tp_ready"], g + 1 + 1)
                    for k in range(KC):
                        act.copy(hT[:, s, k, :], tp[k][:]).then_inc(q["hT_ready"], 1)
                    for r in range(GT):
                        act.wait_ge(q["mx"], g * GT + GT + 1)
                        act.activation(ex[:, r, :], lg[:, r, 0:E], ACT.Exp, bias=neg[:, r:r + 1]
                                       ).then_inc(q["ex_ready"], 1)
                    for f in range(2):
                        act.wait_ge(q["gate_ready"], g * 2 + (f + 1) + 1)
                        act.wait_ge(q["t_done"], g * 2 + 1)
                        act.activation(th[:, f, :], gu[0][0:FH, :], ACT.Tanh, scale=0.5).then_inc(q["th_ready"], 1)
                    act.wait_ge(q["cp_ready"], g + 1 + 1)
                    act.wait_ge(cnt_out[s], b * 16 + 1)
                    act.copy(tot[:, bass.ds(g * GT, GT)].rearrange("e (a r) -> e a r", r=2),
                             cp[:].rearrange("e a (r t) -> e a r t", r=2)[:, :, :, P]).then_inc(q["topk"], 1)
                    act.copy(cnt[:, s].rearrange("e (a r) t -> e a r t", r=2),
                             cp[:].rearrange("e a (r t) -> e a r t", r=2)[:, :, :, 0:P]).then_inc(q["cnt_ready"], 1)

        @block.vector
        def _(v):
            L = 9
            cs = q["group_chain"]
            with v.Fori(0, B) as b:
                for s in range(2):
                    g = b * 2 + s
                    link2 = Chain(v, cs, g * L)
                    v.wait_ge(q["lg_ready"], g + 1 + 1)
                    v.memset(carrier[:], 0.0)
                    for r in range(GT):
                        last = v.max(m8[:, r, :], lg[:, r, 0:E])
                    link2(last)
                    v.wait_ge(q["ex_ready"], g * GT + 1)
                    link2(v.tensor_scalar(neg[:], m8[:, :, 0], -1.0, None, ALU.mult))
                    v.nop().then_inc(q["mx"], GT)
                    v.wait_ge(q["ex_ready"], g * GT + GT + 1)
                    v.memset(carrier[:], 0.0)
                    for r in range(GT):
                        last = v.max(e8[:, r, :], ex[:, r, :])
                    link2(last)
                    link2(v.tensor_reduce(wsum[:], e8[:], AX.X, ALU.add))
                    link2(v.reciprocal(wsum[:], wsum[:]))
                    v.memset(carrier[:], 0.0)
                    for r in range(GT):
                        last = v.match_replace(rep[:, r, :], e8[:, r, :], ex[:, r, :], -1.0)
                    link2(last)
                    v.wait_ge(q["cp_ready"], g + 1)
                    link2(v.tensor_scalar(mask[:], rep[:], 0.0, None, ALU.is_lt))
                    link2(v.tensor_tensor(ex[:], ex[:], mask[:], ALU.mult))
                    link2(v.tensor_tensor(rows[:, s, :, D:ROW], ex[:],
                                          wsum[:].rearrange("p (r o) -> p r o", o=1).broadcast_to([P, GT, E]), ALU.mult))
                    v.nop().then_inc(q["mask_ready"], 1)
                    for f in range(2):
                        v.wait_ge(q["th_ready"], g * 2 + (f + 1) + 1)
                        v.scalar_tensor_tensor(th[:, f, :], th[:, f, :], 1.0, gu[0][0:FH, :], ALU.add, ALU.mult
                                               ).then_inc(q["t_done"], 1)
                        v.wait_ge(q["t_done"], g * 2 + (f + 1) + 1)
                        v.wait_ge(q["up_ready"], g * 2 + (f + 1) + 1)
                        v.wait_ge(q["dn_ready"], g * GT + 1)
                        v.scalar_tensor_tensor(act_in[:, f, :], th[:, f, :], 0.5, gu[1][0:FH, :], ALU.mult, ALU.mult
                                               ).then_inc(q["a_done"], 1)
                    for r in range(GT):
                        n = b * BT + (s * GT + r)
                        xt = m["x"][:, bass.ds(n, 1), :].rearrange("p o d -> p (o d)")
                        v.wait_ge(q["dn_ready"], n + 1 + 1)
                        v.tensor_tensor(xt, xt, gu[2][:, 0:D], ALU.add).then_inc(q["x_done"], 1)
            v.wait_ge(q["topk"], groups + 1)
            v.wait_ge(q["consts"], 3)
            v.tensor_scalar(tot[:], tot[:], 0.5, None, ALU.mult).then_inc(cs, 1)
            v.wait_ge(cs, groups * L + 1 + 1)
            v.tensor_tensor_scan(tot[:], onesE[:], tot[:], 0.0, ALU.mult, ALU.add).then_inc(q["chain"], 1)


def experts(nc, w_gate, w_up, w_down, rows_dram, counts_dram, ends_dram, out):
    R = 4
    with ExitStack() as c:
        def sb(name, shape, dt=F32):
            return c.enter_context(nc.sbuf_tensor("ex_" + name, shape, dt))

        sems = []

        def sem(name):
            sems.append(c.enter_context(nc.semaphore("ex_" + name)))
            return sems[-1]

        ident = sb("ident2", [P, P])
        ends, le = sb("ends", [P, E, TILES]), sb("le", [P, E, TILES])
        carrier, zero = sb("carrier", [P, 3 * R + 1]), sb("zero", [P, 1])
        slot, tok = sb("slot", [P, 1]), sb("tok", [P, P])
        tile_of, first, none, goal = sb("tile_of", [P, E]), sb("first", [P, E]), sb("none", [P, E]), sb("goal", [P, E])
        row_f, base = sb("row_f", [P, E]), sb("base", [P, E])
        row_id, tok_id = sb("row_id", [P, E], U32), sb("tok_id", [P, E], U32)
        eoff = sb("eoff", [P, E])
        row_cur, tok_cur = sb("row_cur", [P, R], U32), sb("tok_cur", [P, R], U32)
        vr, junk, pos = sb("vr", [P, R, P]), sb("junk", [P, R, P]), sb("pos", [P, R])
        WGU, WD = sb("wgu", [P, R, 2, KC, F]), sb("wd", [FH, R, 2, D])
        xg, xT = sb("xg", [P, R, ROW]), sb("xT", [P, 2, KC, P])
        th, t2, aT, yw = sb("th", [FH, 2, 2, P]), sb("t2", [FH, 2, 2, P]), sb("aT", [FH, 2, 2, P]), sb("yw", [P, R, D])
        tp = [c.enter_context(nc.psum_tensor(f"ex_tp{k}", [P, 512], F32)) for k in range(2)]
        gu = [c.enter_context(nc.psum_tensor(f"ex_gu{k}", [P, 4, P], F32)) for k in range(2)]
        yp = [c.enter_context(nc.psum_tensor(f"ex_yp{k}", [P, 512], F32)) for k in range(2)]
        names = ("ends_in consts chain ids row_copied pos_done pos_copied tok_copied tp_ready xT_ready gu_ready "
                 "th_ready t2_ready a_ready y_ready yw_ready id0 carried").split()
        q = {n: sem(n) for n in names}
        w_in, v_in, x_in, added = ([sem(f"{n}{s}") for s in range(R)] for n in ("w_in", "v_in", "x_in", "added"))
        prime(nc, sems[:len(names)])
        block = c.enter_context(nc.Block())

        @block.sync
        def _(sp):
            sp.dma_start(ends[:].rearrange("p e n -> p (e n)"), ends_dram.broadcast_to([P, E * TILES])).then_inc(q["ends_in"], 16)
            with sp.Fori(0, E // R) as it:
                for s in range(R):
                    e = it * R + s
                    sp.wait_ge(q["y_ready"], it * R + 1)
                    for g, w in enumerate((w_gate, w_up)):
                        sp.dma_start(WGU[:, s, g], w[bass.ds(e, 1)].rearrange("o (k p) f -> p (o k) f", p=P)
                                     ).then_inc(w_in[s], 16)
                    sp.dma_start(WD[:, s], w_down[bass.ds(e, 1)].rearrange("o (k p) f -> p (o k) f", p=FH)
                                 ).then_inc(w_in[s], 16)

        @block.gpsimd
        def _(pool):
            def carry(at):
                pool.tensor_tensor(carrier[:, at:at + 1], zero[:], zero[:], ALU.add).then_inc(q["carried"], 1)

            pool.memset(zero[:], 0.0).then_inc(q["consts"], 1)
            pool.wait_ge(q["consts"], 2)
            pool.memset(ident[:], 0.0).then_inc(q["id0"], 1)
            pool.wait_ge(q["id0"], 2)
            pool.affine_select(out=ident[:], in_=ident[:], compare_op=ALU.not_equal, fill=1.0,
                               base=0, pattern=[[-1, P]], channel_multiplier=1).then_inc(q["consts"], 1)
            pool.iota(slot[:], pattern=[[0, 1]], base=0, channel_multiplier=1,
                      allow_small_or_imprecise_dtypes=True).then_inc(q["consts"], 1)
            pool.iota(tok[:], pattern=[[1, P]], base=0, channel_multiplier=0,
                      allow_small_or_imprecise_dtypes=True).then_inc(q["consts"], 1)
            pool.iota(eoff[:], pattern=[[TILES, E]], base=0, channel_multiplier=0,
                      allow_small_or_imprecise_dtypes=True).then_inc(q["consts"], 1)
            with pool.Fori(0, E // R) as it:
                for s in range(R):
                    pool.wait_ge(q["row_copied"], it * R + (s + 1) + 1)
                    pool.wait_ge(q["pos_done"], it * R + 1)
                    carry(s)
                    pool.indirect_dma_start(
                        out=vr[:, s], out_offset=None, in_=counts_dram,
                        in_offset=bass.IndirectOffsetOnAxis(ap=row_cur[:, s:s + 1], axis=0),
                        bounds_check=E * TILES - 1).then_inc(v_in[s], 16)
            with pool.Fori(0, E // R) as it:
                for s in range(R):
                    pool.wait_ge(q["tok_copied"], it * R + (s + 1) + 1)
                    pool.wait_ge(q["yw_ready"], it * R + 1)
                    carry(R + s)
                    pool.indirect_dma_start(
                        out=xg[:, s], out_offset=None, in_=rows_dram,
                        in_offset=bass.IndirectOffsetOnAxis(ap=tok_cur[:, s:s + 1], axis=0),
                        bounds_check=NT + P - 1).then_inc(x_in[s], 16)
                for s in range(R):
                    pool.wait_ge(q["yw_ready"], it * R + (s + 1) + 1)
                    if s:
                        pool.wait_ge(added[s - 1], it * 16 + 16)
                    carry(2 * R + s)
                    pool.indirect_dma_start(
                        out=out, out_offset=bass.IndirectOffsetOnAxis(ap=tok_cur[:, s:s + 1], axis=0),
                        in_=yw[:, s], in_offset=None, bounds_check=NT + P - 1, compute_op=ALU.add
                    ).then_inc(added[s], 16)
                pool.wait_ge(added[R - 1], it * 16 + 16)
                carry(3 * R)
            pool.wait_ge(added[R - 1], 16 * (E // R))

        @block.tensor
        def _(pe):
            pe.wait_ge(q["consts"], 3)
            with pe.Fori(0, E // R) as it:
                for s in range(R):
                    d = s % 2
                    e = it * R + s
                    pe.wait_ge(x_in[s], it * 16 + 16)
                    if s >= 2:
                        pe.wait_ge(q["xT_ready"], e - 1 + 1)
                    else:
                        pe.wait_ge(q["xT_ready"], it * R + 1)
                    for k in range(KC):
                        last = pe.transpose(tp[d][:, k * P:(k + 1) * P], xg[:, s, k * P:(k + 1) * P], ident[:])
                    last.then_inc(q["tp_ready"], 1)
                    pe.wait_ge(w_in[s], it * 48 + 48)
                    pe.wait_ge(q["xT_ready"], e + 1 + 1)
                    pe.wait_ge(q["a_ready"], (e - 1 if s >= 2 else it * R) + 1)
                    for g in range(2):
                        for f in range(2):
                            for k in range(KC):
                                last = pe.matmul(gu[d][0:FH, g * 2 + f, :], WGU[:, s, g, k, f * FH:(f + 1) * FH],
                                                 xT[:, d, k, :], start=k == 0, stop=k == KC - 1)
                    last.then_inc(q["gu_ready"], 1)
                    pe.wait_ge(q["a_ready"], e + 1 + 1)
                    pe.wait_ge(q["yw_ready"], (e - 1 if s >= 2 else it * R) + 1)
                    for f in range(2):
                        last = pe.matmul(yp[d][:, 0:D], aT[:, d, f, :], WD[:, s, f, :], start=f == 0, stop=f == 1)
                    last.then_inc(q["y_ready"], 1)

        @block.scalar
        def _(act):
            with act.Fori(0, E // R) as it:
                for s in range(R):
                    d = s % 2
                    e = it * R + s
                    act.wait_ge(q["tp_ready"], e + 1 + 1)
                    act.wait_ge(q["gu_ready"], (e - 1 if s >= 2 else it * R) + 1)
                    act.copy(xT[:, d].rearrange("p k t -> p (k t)"), tp[d][:, 0:KC * P]).then_inc(q["xT_ready"], 1)
                    act.wait_ge(q["gu_ready"], e + 1 + 1)
                    act.wait_ge(q["t2_ready"], (e - 1 if s >= 2 else it * R) + 1)
                    act.activation(th[:, d], gu[d][0:FH, 0:2, :], ACT.Tanh, scale=0.5).then_inc(q["th_ready"], 1)
                    act.wait_ge(q["y_ready"], e + 1 + 1)
                    act.wait_ge(q["carried"], it * (2 * R + 1) + E + 1)
                    act.activation(yw[:, s], yp[d][:, 0:D], ACT.Copy, scale=xg[:, s, bass.ds(e + D, 1)]
                                   ).then_inc(q["yw_ready"], 1)

        @block.vector
        def _(v):
            link = Chain(v, q["chain"])
            v.wait_ge(q["ends_in"], 17)
            v.wait_ge(q["consts"], 6)
            sc = slot[:, 0:1]
            link(v.tensor_scalar(le[:], ends[:], sc, None, ALU.is_le))
            link(v.tensor_reduce(tile_of[:], le[:], AX.X, ALU.add))
            link(v.tensor_tensor(le[:], le[:], ends[:], ALU.mult))
            link(v.tensor_reduce(first[:], le[:], AX.X, ALU.max))
            link(v.tensor_scalar(none[:], tile_of[:], float(TILES), None, ALU.is_ge))
            link(v.tensor_scalar(goal[:], first[:], sc, -2.0, ALU.subtract, ALU.mult))
            link(v.tensor_scalar(goal[:], goal[:], 1.0, None, ALU.add))
            link(v.scalar_tensor_tensor(goal[:], none[:], -4.0 * NT, goal[:], ALU.mult, ALU.add))
            link(v.tensor_scalar(row_f[:], tile_of[:], float(TILES - 1), None, ALU.min))
            link(v.tensor_tensor(row_f[:], row_f[:], eoff[:], ALU.add))
            link(v.tensor_copy(row_id[:], row_f[:]))
            link(v.tensor_scalar(base[:], none[:], sc, None, ALU.mult))
            link(v.scalar_tensor_tensor(base[:], tile_of[:], float(P), base[:], ALU.mult, ALU.add))
            with v.Fori(0, E // R) as it:
                for s in range(R):
                    v.wait_ge(q["carried"], it * R + 1)
                    v.tensor_copy(row_cur[:, s:s + 1], row_id[:, bass.ds(it * R + s, 1)]).then_inc(q["row_copied"], 1)
                for s in range(R):
                    v.wait_ge(v_in[s], it * 16 + 16)
                    v.scalar_tensor_tensor(junk[:, s], vr[:, s], goal[:, bass.ds(it * R + s, 1)], tok[:], ALU.is_equal,
                                           ALU.mult, accum_out=pos[:, s:s + 1]).then_inc(q["pos_done"], 1)
                    v.wait_ge(q["pos_done"], it * R + (s + 1) + 1)
                    v.tensor_tensor(tok_id[:, bass.ds(it * R + s, 1)], pos[:, s:s + 1], base[:, bass.ds(it * R + s, 1)],
                                    ALU.add).then_inc(q["ids"], 1)
            v.wait_ge(q["ids"], E + 1)
            with v.Fori(0, E // R) as it:
                for s in range(R):
                    v.wait_ge(q["carried"], it * (2 * R + 1) + E + 1)
                    v.tensor_copy(tok_cur[:, s:s + 1], tok_id[:, bass.ds(it * R + s, 1)]).then_inc(q["tok_copied"], 1)
                for s in range(R):
                    d = s % 2
                    e = it * R + s
                    v.wait_ge(q["th_ready"], e + 1 + 1)
                    v.scalar_tensor_tensor(t2[:, d], th[:, d], 1.0, gu[d][0:FH, 0:2, :], ALU.add, ALU.mult
                                           ).then_inc(q["t2_ready"], 1)
                    v.wait_ge(q["t2_ready"], e + 1 + 1)
                    v.wait_ge(q["y_ready"], (e - 1 if s >= 2 else it * R) + 1)
                    v.scalar_tensor_tensor(aT[:, d], t2[:, d], 0.5, gu[d][0:FH, 2:4, :], ALU.mult, ALU.mult
                                           ).then_inc(q["a_ready"], 1)


_INS = ['L0_attn_x', 'L0_attn_ln_g', 'L0_attn_ln_b', 'L0_attn_w_qkvb', 'L0_attn_b_qkvb', 'L0_attn_w_out',
        'L0_attn_b_out', 'L0_ffn_router_w', 'L0_ffn_w_gate', 'L0_ffn_w_up', 'L0_ffn_w_down',
        'L0_ffn_ws_gate_up', 'L0_ffn_ws_down']


def kernel(**inputs):
    import numpy as _np
    import concourse.bacc as _bacc
    from concourse import mybir as _mybir
    from concourse.bass_utils import run_bass_kernel_spmd as _run

    nc = _bacc.Bacc("TRN2", target_bir_lowering=False, num_devices=1)
    arrays, args = {}, []
    for name in _INS:
        a = _np.ascontiguousarray(inputs[name])
        arrays[f"in_{name}_dram"] = a
        args.append(nc.dram_tensor(f"in_{name}_dram", a.shape, _mybir.dt.from_np(a.dtype), kind="ExternalInput").ap())
    args.append(nc.dram_tensor("out_0_dram", (NT + P, D), F32, kind="ExternalOutput").ap())
    build(nc, *args)
    r = _run(nc, [arrays], core_ids=[0])
    return r.results[0]["out_0_dram"][0:NT].reshape(B, T, D)
```

```python
import concourse.bass as bass
from concourse import mybir
from contextlib import ExitStack

F32 = mybir.dt.float32
BF16 = mybir.dt.bfloat16
U32 = mybir.dt.uint32
ALU = mybir.AluOpType
ACT = mybir.ActivationFunctionType
AX = mybir.AxisListType

B, T, D = 8, 1024, 256
NH, HD = 16, 16
NT = B * T
P = 128
TILES = NT // P
BT = T // P
KC = D // P
GT = 4
GN = GT * P
GROUPS = TILES // GT
PROJ = 4 * D
PC = PROJ // P
E, TOPK, CAP, F = 64, 8, 128, 192
FH = F // 2
ROW = D + E
EPS, NORM_EPS = 1e-5, 1e-6
WIN = 64
MB = 4
NWIN = T // WIN


class Chain:

    def __init__(self, eng, sem, base=0, first=1):
        self.eng, self.sem, self.base, self.first, self.n = eng, sem, base, first, 0

    def __call__(self, ins):
        ins.then_inc(self.sem, 1)
        self.n += 1
        self.eng.wait_ge(self.sem, self.base + self.n + self.first)


def mid(ap, count):
    return ap.rearrange("p (o n) -> p o n", o=1).broadcast_to([ap.shape[0], count, ap.shape[1]])


def prime(nc, sems):
    with nc.Block() as block:
        @block.sync
        def _(sp):
            for s in sems:
                sp.nop().then_inc(s, 1)


def build(nc, x, ln_g, ln_b, w_qkvb, b_qkvb, w_out, b_out, router_w, w_gate, w_up, w_down, ws_gate_up,
          ws_down, out):
    scratch = [nc.dram_tensor(n, s, F32, kind="Internal").ap() for n, s in (
        ("lanes_dram", (B, PROJ, T)), ("scan_dram", (B, D, T)), ("rows_dram", (NT + P, ROW)),
        ("counts_dram", (E * TILES, P)), ("ends_dram", (1, E * TILES)))]
    lanes_dram, scan_dram, rows_dram, counts_dram, ends_dram = scratch
    with ExitStack() as keep:
        def sb(name, shape, dt=F32):
            return keep.enter_context(nc.sbuf_tensor(name, shape, dt))

        m = {
            "x": sb("x_sb", [P, TILES, D]),
            "ident": sb("ident", [P, P]),
            "mu": sb("mu", [P, TILES]), "var": sb("var", [P, TILES]),
            "stats": sb("stats", [P, TILES, 6]),
            "r1": sb("r1", [P, TILES]), "r12": sb("r12", [P, TILES]), "shift": sb("shift", [P, TILES]),
            "rs1": sb("rs1", [P, TILES]), "shift1": sb("shift1", [P, TILES]),
            "tmp": sb("tmp", [P, TILES]), "tmp2": sb("tmp2", [P, TILES]),
        }
        moments(nc, m, x)
        project(nc, m, ln_g, ln_b, w_qkvb, b_qkvb, lanes_dram)
        scan(nc, m, lanes_dram, scan_dram)
        attn_out(nc, m, scan_dram, w_out, b_out)
        route(nc, m, router_w, ws_gate_up, ws_down, rows_dram, counts_dram, ends_dram, out)
    experts(nc, w_gate, w_up, w_down, rows_dram, counts_dram, ends_dram, out)


def row_moments(v, link, m):
    half = lambda i: m["stats"][:, :, i]
    link(v.tensor_tensor(m["mu"][:], half(1), half(4), ALU.add))
    link(v.tensor_tensor(m["tmp"][:], half(1), half(4), ALU.subtract))
    link(v.tensor_scalar(m["mu"][:], m["mu"][:], 0.5, None, ALU.mult))
    link(v.tensor_scalar(m["tmp"][:], m["tmp"][:], 0.5, None, ALU.mult))
    link(v.tensor_tensor(m["tmp"][:], m["tmp"][:], m["tmp"][:], ALU.mult))
    link(v.tensor_tensor(m["var"][:], half(2), half(5), ALU.add))
    link(v.scalar_tensor_tensor(m["var"][:], m["var"][:], 1.0 / D, m["tmp"][:], ALU.mult, ALU.add))


def moments(nc, m, x):
    with ExitStack() as c:
        x_in, stat, chain, need_sqrt, have_sqrt, id0 = (
            c.enter_context(nc.semaphore("mo_" + n)) for n in ("x_in", "stat", "chain", "need_sqrt", "have_sqrt", "id0"))
        eps = c.enter_context(nc.sbuf_tensor("mo_eps", [P, 1], F32))
        block = c.enter_context(nc.Block())

        @block.sync
        def _(sp):
            for b in range(B):
                sp.dma_start(m["x"][:, b * BT:(b + 1) * BT, :],
                             x[b].rearrange("(n p) d -> p n d", p=P)).then_inc(x_in, 16)

        @block.gpsimd
        def _(pool):
            pool.memset(m["ident"][:], 0.0).then_inc(id0, 1)
            pool.wait_ge(id0, 1)
            pool.affine_select(out=m["ident"][:], in_=m["ident"][:], compare_op=ALU.not_equal, fill=1.0,
                               base=0, pattern=[[-1, P]], channel_multiplier=1).then_inc(id0, 1)

        @block.scalar
        def _(act):
            act.wait_ge(need_sqrt, 1)
            act.activation(m["r1"][:], m["var"][:], ACT.Sqrt, bias=eps[:]).then_inc(have_sqrt, 1)
            act.wait_ge(need_sqrt, 2)
            act.activation(m["r12"][:], m["tmp"][:], ACT.Sqrt, bias=eps[:]).then_inc(have_sqrt, 1)

        @block.vector
        def _(v):
            link = Chain(v, chain, first=0)
            link(v.memset(eps[:], EPS))
            v.wait_ge(x_in, 16 * B)
            with v.Fori(0, B) as b:
                for r in range(BT):
                    n = b * BT + r
                    v.bn_stats(m["stats"][:, bass.ds(n, 1), :].rearrange("p o s -> p (o s)"),
                               m["x"][:, bass.ds(n, 1), :].rearrange("p o d -> p (o d)")).then_inc(stat, 1)
            v.wait_ge(stat, TILES)
            row_moments(v, link, m)
            v.nop().then_inc(need_sqrt, 1)
            v.wait_ge(have_sqrt, 1)
            link(v.reciprocal(m["r1"][:], m["r1"][:]))
            link(v.tensor_tensor(m["tmp"][:], m["var"][:], m["r1"][:], ALU.mult))
            link(v.tensor_tensor(m["tmp"][:], m["tmp"][:], m["r1"][:], ALU.mult))
            v.nop().then_inc(need_sqrt, 1)
            v.wait_ge(have_sqrt, 2)
            link(v.reciprocal(m["r12"][:], m["r12"][:]))
            link(v.tensor_tensor(m["r12"][:], m["r12"][:], m["r1"][:], ALU.mult))
            link(v.scalar_tensor_tensor(m["shift"][:], m["mu"][:], -1.0, m["r12"][:], ALU.mult, ALU.mult))
            link(v.scalar_tensor_tensor(m["shift1"][:], m["mu"][:], -1.0, m["r1"][:], ALU.mult, ALU.mult))
            link(v.tensor_scalar(m["rs1"][:], m["r1"][:], 1.0, None, ALU.add))


def project(nc, m, ln_g, ln_b, w_qkvb, b_qkvb, lanes_dram):
    with ExitStack() as c:
        def sb(name, shape, dt=F32):
            return c.enter_context(nc.sbuf_tensor("pj_" + name, shape, dt))

        sems = []

        def sem(name):
            sems.append(c.enter_context(nc.semaphore("pj_" + name)))
            return sems[-1]

        W = sb("w_qkvb_sb", [P, KC, PROJ])
        bias, gain, off = sb("bias", [P, PC]), sb("gain", [P, KC]), sb("off", [P, KC])
        xh, nT, stage = sb("xh", [P, GT, D]), sb("nT", [P, 2, KC, GN]), sb("stage", [P, 2, PC, GN])
        tp = [c.enter_context(nc.psum_tensor(f"pj_tp{k}", [P, GN], F32)) for k in range(KC)]
        pj = [c.enter_context(nc.psum_tensor(f"pj_pj{k}", [P, GN], F32)) for k in range(4)]
        w_in, xh_ready, tp_ready, nT_ready, pj_ready, dve_out, act_out = map(sem, (
            "w_in", "xh_ready", "tp_ready", "nT_ready", "pj_ready", "dve_out", "act_out"))
        stored = [sem("stored0"), sem("stored1")]
        LOADS = 4 * (KC + 2) + 2
        prime(nc, sems)
        block = c.enter_context(nc.Block())

        @block.sync
        def _(sp):
            for a in range(4):
                for k in range(KC):
                    sp.dma_start(W[:, k, :].rearrange("p (h a j) -> p h a j", a=4, j=HD)[:, :, a, :],
                                 w_qkvb[k * P:(k + 1) * P, a * D:(a + 1) * D].rearrange("p (h j) -> p h j", j=HD)
                                 ).then_inc(w_in, 16)
                for h in range(2):
                    row = h * 4 * HD + a * HD
                    sp.dma_start(bias[row:row + HD, :],
                                 b_qkvb[a * D:(a + 1) * D].rearrange("(c h j) -> h j c", h=2, j=HD)[h],
                                 allow_slow_non_contiguous=True).then_inc(w_in, 16)
            sp.dma_start(gain[:], ln_g.rearrange("(c p) -> p c", p=P), allow_slow_non_contiguous=True).then_inc(w_in, 16)
            sp.dma_start(off[:], ln_b.rearrange("(c p) -> p c", p=P), allow_slow_non_contiguous=True).then_inc(w_in, 16)
            with sp.Fori(0, B) as b:
                for s in range(2):
                    sp.wait_ge(dve_out, b * 8 + 4 * (s + 1) + 1)
                    sp.wait_ge(act_out, b * 8 + 4 * (s + 1) + 1)
                    sp.dma_start(lanes_dram[bass.ds(b, 1), :, s * GN:(s + 1) * GN].rearrange("o (c p) t -> p (o c) t", p=P),
                                 stage[:, s]).then_inc(stored[s], 16)
            sp.wait_ge(stored[0], 16 * B + 1)
            sp.wait_ge(stored[1], 16 * B + 1)

        @block.vector
        def _(v):
            v.wait_ge(w_in, 16 * LOADS + 1)
            with v.Fori(0, B) as b:
                for s in range(2):
                    v.wait_ge(tp_ready, b * 2 + s + 1)
                    for r in range(GT):
                        n = b * BT + (s * GT + r)
                        v.tensor_scalar(xh[:, r, :], m["x"][:, bass.ds(n, 1), :].rearrange("p o d -> p (o d)"),
                                        m["r12"][:, bass.ds(n, 1)], m["shift"][:, bass.ds(n, 1)],
                                        ALU.mult, ALU.add).then_inc(xh_ready, 1)
                    v.wait_ge(stored[s], b * 16 + 1)
                    for k in range(4):
                        v.wait_ge(pj_ready, b * 16 + (8 * s + k + 1) + 1)
                        v.tensor_scalar(stage[:, s, k, :], pj[k][:], bias[:, k:k + 1], None,
                                        ALU.add).then_inc(dve_out, 1)

        @block.scalar
        def _(act):
            act.wait_ge(w_in, 16 * LOADS + 1)
            with act.Fori(0, B) as b:
                for s in range(2):
                    act.wait_ge(tp_ready, b * 2 + (s + 1) + 1)
                    act.wait_ge(pj_ready, b * 16 + 8 * s + 1)
                    for k in range(KC):
                        act.activation(nT[:, s, k, :], tp[k][:], ACT.Identity, bias=off[:, k:k + 1],
                                       scale=gain[:, k:k + 1]).then_inc(nT_ready, 1)
                    act.wait_ge(stored[s], b * 16 + 1)
                    for k in range(4, PC):
                        act.wait_ge(pj_ready, b * 16 + (8 * s + k + 1) + 1)
                        act.activation(stage[:, s, k, :], pj[k % 4][:], ACT.Identity,
                                       bias=bias[:, k:k + 1]).then_inc(act_out, 1)

        @block.tensor
        def _(pe):
            with pe.Fori(0, B) as b:
                for s in range(2):
                    pe.wait_ge(nT_ready, b * 4 + 2 * s + 1)
                    pe.wait_ge(xh_ready, b * 8 + 4 * (s + 1) + 1)
                    for r in range(GT):
                        for k in range(KC):
                            last = pe.transpose(tp[k][:, r * P:(r + 1) * P], xh[:, r, k * P:(k + 1) * P],
                                                m["ident"][:])
                    last.then_inc(tp_ready, 1)
                    pe.wait_ge(nT_ready, b * 4 + 2 * (s + 1) + 1)
                    for k in range(PC):
                        if k < 4:
                            pe.wait_ge(act_out, b * 8 + 4 * s + 1)
                        else:
                            pe.wait_ge(dve_out, b * 8 + (4 * s + k - 3) + 1)
                        for j in range(KC):
                            last = pe.matmul(pj[k % 4][:], W[:, j, k * P:(k + 1) * P], nT[:, s, j, :],
                                             start=j == 0, stop=j == KC - 1)
                        last.then_inc(pj_ready, 1)


def scan(nc, m, lanes_dram, scan_dram):
    with ExitStack() as c:
        sems = []

        def sb(name, shape, dt=F32):
            return c.enter_context(nc.sbuf_tensor("sc_" + name, shape, dt))

        def pb(name, shape):
            return c.enter_context(nc.psum_tensor("sc_" + name, shape, F32))

        def sem(name):
            sems.append(c.enter_context(nc.semaphore("sc_" + name)))
            return sems[-1]

        HI = HD // 2
        NB = WIN // MB
        QB = NB // 4
        BLOCKS = T // MB
        PAIRS = MB * (MB - 1) // 2
        R = 4
        OPS = 6
        q_, k_, v_, b_ = range(4)
        lanes = sb("lanes", [P, 2, 4, HD, WIN])
        prod, outer = sb("prod", [P, 2, MB, HI, HD]), sb("outer", [P, 2, MB, HI, HD])
        ret, diff, bd = (sb(n, [P, 2, MB, HI]) for n in ("ret", "diff", "bd"))
        xprod = sb("xprod", [P, 2, MB, HI, MB])
        U = sb("U", [P, R, MB, HD])
        X = sb("X", [P, HD, NB, MB * MB])
        sq, ss, inv, power = sb("sq", [P, HD, WIN]), sb("ss", [P, WIN]), sb("inv", [P, WIN]), sb("power", [P, WIN])
        gprod, G = sb("gprod", [P, PAIRS, HD, NB]), sb("G", [P, PAIRS, NB])
        hprod, H = sb("hprod", [P, PAIRS + MB, HD, NB]), sb("H", [P, PAIRS + MB, NB])
        KQ = sb("KQ", [P, 2, NB, MB * MB])
        N2, T2 = sb("N2", [P, HD, NB, 2]), sb("T2", [P, HD, NB, 2])
        N3, T3 = sb("N3", [P, HD, NB]), sb("T3", [P, HD, NB])
        Sc = sb("Sc", [P, R, HD, HD])
        sqp, sqh = sb("sqp", [P, 2, MB, HD, HD]), sb("sqh", [P, R, MB, HD, HD // 2])
        uq = sb("uq", [P, R, MB, MB, HD])
        ow = sb("ow", [P, 2, HD, WIN])
        zero = sb("zero", [P, HI * HD])
        S = [pb(f"S{h}", [P, 512]) for h in range(2)]
        O = [pb(f"O{h}", [P, 512]) for h in range(2)]
        (step0, step1, outer_ready0, outer_ready1, S_ready, Sc_ready, u_ready, sqp_ready, o_in_ready, o_ready, ow_ready,
         sq_ready, ss_ready, inv_ready, k_ready, g_ready, chain, x_ready, H_ready, KQ_ready, beta_ready, consts
         ) = map(sem, ("step0 step1 outer0 outer1 S_ready Sc_ready u_ready sqp_ready o_in_ready o_ready ow_ready sq_ready "
                       "ss_ready inv_ready k_ready g_ready chain x_ready H_ready KQ_ready beta_ready consts"
                       ).split())
        step = [step0, step1]
        outer_ready = [outer_ready0, outer_ready1]
        loaded, stored = [sem("loaded0"), sem("loaded1")], [sem("out0"), sem("out1")]
        prime(nc, sems)
        block = c.enter_context(nc.Block())
        CH = 14

        def lag_of(ap, lag):
            return ap[..., lag * MB:MB * MB:MB + 1]

        def first_pair(lag, with_zero):
            lags = range(0 if with_zero else 1, lag)
            return sum(MB - x for x in lags)

        def steps(s, kind, lo, hi):
            return lanes[:, s, kind].rearrange("p j (n a) -> p j n a", a=MB)[:, :, :, lo:hi]

        @block.sync
        def _(sp):
            def load(w, s):
                sp.dma_start(lanes[:, s].rearrange("p a j t -> p (a j) t"),
                             lanes_dram.rearrange("b (h r) t -> (b h) r t", h=NH)[:, :, bass.ds(w * WIN, WIN)]
                             ).then_inc(loaded[s], 16)

            def store(w, s):
                sp.wait_ge(ow_ready, w * NB + (NB + 1))
                sp.dma_start(scan_dram.rearrange("b (h i) t -> (b h) i t", i=HD)[:, :, bass.ds(w * WIN, WIN)],
                             ow[:, s]).then_inc(stored[s], 16)

            load(0, 0)
            load(1, 1)
            with sp.Fori(0, NWIN // 2 - 1) as p:
                for s in range(2):
                    w = p * 2 + s
                    sp.wait_ge(outer_ready[1], w * NB + (NB + 1))
                    sp.wait_ge(o_in_ready, w * NB + (NB + 1))
                    load(w + 2, s)
                    store(w, s)
            for s in range(2):
                store(NWIN - 2 + s, s)
            for s in range(2):
                sp.wait_ge(stored[s], 16 * (NWIN // 2) + 1)

        @block.scalar
        def _(act):
            def begin(w, s, p):
                act.wait_ge(loaded[s], p * 16 + 17)
                act.wait_ge(ss_ready, w + 1)
                act.activation(lanes[:, s, b_], lanes[:, s, b_], ACT.Sigmoid).then_inc(beta_ready, 1)
                act.activation(sq[:], lanes[:, s, k_], ACT.Square).then_inc(sq_ready, 1)

            def finish(w, s):
                act.wait_ge(H_ready, w + 2)
                for lag in range(MB):
                    at = first_pair(lag, True)
                    act.copy(lag_of(KQ[:, s], lag), H[:, at:at + MB - lag, :].rearrange("p c n -> p n c")
                             ).then_inc(KQ_ready, 1)

            def quarter(w, s, q, p):
                for i in range(QB):
                    n = w * NB + (q * QB + i)
                    at = n if isinstance(n, int) else None
                    for h in range(2):
                        act.wait_ge(step[h], n * (OPS - 1) + 2)
                        if at is None or at >= R:
                            act.wait_ge(o_in_ready, n - R + 2)
                        act.copy(Sc[:, (q * QB + i) % R, h * HI:(h + 1) * HI, :].rearrange("p i j -> p (i j)"),
                                 S[h][:, 0:HI * HD]).then_inc(Sc_ready, 1)
                    if at is None or at >= 3:
                        evacuate(w, s, q * QB + i - 3, n - 3, p)

            def evacuate(w, s, i, n, p):
                so, io = (s, i) if i >= 0 else (1 - s, i + NB)
                act.wait_ge(o_ready, n + 2)
                if i == 0:
                    act.wait_ge(stored[s], p * 16 + 1)
                act.copy(ow[:, so, :, io * MB:(io + 1) * MB].rearrange("p i t -> p t i"),
                         O[io % 2][:, 0:MB * HD].rearrange("p (t i) -> p t i", i=HD)).then_inc(ow_ready, 1)

            def window(w, s, p, last=False, pn=None):
                for q in range(4):
                    quarter(w, s, q, p)
                    if q == 0 and not last:
                        begin(w + 1, 1 - s, p + s)
                if not last:
                    finish(w + 1, 1 - s)

            act.wait_ge(consts, 2)
            begin(0, 0, 0)
            finish(0, 0)
            window(0, 0, 0)
            window(1, 1, 0)
            with act.Fori(1, NWIN // 2 - 1) as p:
                for s in range(2):
                    window(p * 2 + s, s, p)
            window(NWIN - 2, 0, NWIN // 2 - 1)
            window(NWIN - 1, 1, NWIN // 2 - 1, last=True)
            for i in range(3):
                evacuate(NWIN - 1, 1, NB - 3 + i, BLOCKS - 3 + i, NWIN // 2 - 1)

        @block.tensor
        def _(pe):
            def update(n, slot):
                for h in range(2):
                    pe.wait_ge(outer_ready[h], n + 2)
                    pe.wait_ge(Sc_ready, n * 2 + (h + 2))
                    for t in range(MB):
                        last = pe.matmul(S[h][:, 0:HI * HD], m["ident"][:], outer[:, h, t].rearrange("p i j -> p (i j)"),
                                         start=False, stop=t == MB - 1, skip_group_check=True)
                    last.then_inc(S_ready, 1)

            def outputs(n, slot):
                pe.wait_ge(o_in_ready, n + 2)
                if not isinstance(n, int) or n >= 2:
                    pe.wait_ge(ow_ready, n)
                for j in range(HD // 2):
                    pe.matmul(O[slot % 2][:, 0:MB * HD], m["ident"][:],
                              sqh[:, slot].rearrange("p t i j -> p (t i) j")[:, :, j], start=j == 0, stop=False)
                for x in range(MB):
                    last = pe.matmul(O[slot % 2][:, 0:MB * HD], m["ident"][:], uq[:, slot, :, x, :],
                                     start=False, stop=x == MB - 1)
                last.then_inc(o_ready, 1)

            pe.wait_ge(consts, 3)
            for h in range(2):
                pe.matmul(S[h][:, 0:HI * HD], m["ident"][:], zero[:], start=True, stop=True).then_inc(S_ready, 1)
            for n in range(R):
                update(n, n)
                if n >= 2:
                    outputs(n - 2, n - 2)
            with pe.Fori(1, BLOCKS // R) as it:
                for r in range(R):
                    update(it * R + r, r)
                    outputs(it * R + (r - 2), (r - 2) % R)
            for n in range(BLOCKS - 2, BLOCKS):
                outputs(n, n % R)

        @block.gpsimd
        def _(pool):
            pool.memset(zero[:], 0.0).then_inc(consts, 1)
            pool.memset(KQ[:], 0.0).then_inc(consts, 1)
            pool.memset(power[:], -0.5).then_inc(chain, 1)
            pool.wait_ge(chain, 2)
            pool.wait_ge(consts, 3)

            def norms(w, s):
                pool.wait_ge(ss_ready, w + 2)
                pool.tensor_tensor(inv[:], ss[:], power[:], ALU.pow).then_inc(inv_ready, 1)

            def pairs(w, s):
                pool.wait_ge(k_ready, w + 2)
                for lag in range(1, MB):
                    at = first_pair(lag, False)
                    last = pool.tensor_tensor(gprod[:, at:at + MB - lag].rearrange("p c j n -> p j n c"),
                                              steps(s, k_, lag, MB), steps(s, k_, 0, MB - lag), ALU.mult)
                for lag in range(MB):
                    at = first_pair(lag, True)
                    last = pool.tensor_tensor(hprod[:, at:at + MB - lag].rearrange("p c j n -> p j n c"),
                                              steps(s, q_, lag, MB), steps(s, k_, 0, MB - lag), ALU.mult)
                last.then_inc(g_ready, 1)

            def quarter(w, s, q):
                for i in range(QB):
                    b = q * QB + i
                    n = w * NB + b
                    r = b % R
                    pool.wait_ge(Sc_ready, n * 2 + 3)
                    pool.tensor_tensor(sqp[:, b % 2].rearrange("p t i j -> p t i j"),
                                       Sc[:, r].rearrange("p i j -> p (i j)").rearrange("p (o x) -> p o x", o=1).broadcast_to([P, MB, HD * HD]).rearrange("p t (i j) -> p t i j", j=HD),
                                       lanes[:, s, q_, :, b * MB:(b + 1) * MB].rearrange("p j (t o) -> p t o j", o=1)
                                       .broadcast_to([P, MB, HD, HD]), ALU.mult).then_inc(sqp_ready, 1)
                    pool.wait_ge(sqp_ready, n + 2)
                    if not isinstance(n, int) or n >= R:
                        pool.wait_ge(o_ready, n - R + 2)
                    pool.tensor_tensor(sqh[:, r], sqp[:, b % 2, :, :, 0:HD // 2], sqp[:, b % 2, :, :, HD // 2:HD],
                                       ALU.add)
                    pool.wait_ge(u_ready, n * 2 + 3)
                    if b == 0:
                        pool.wait_ge(KQ_ready, w * MB + (MB + 1))
                    pool.tensor_tensor(uq[:, r],
                                       U[:, r].rearrange("p s i -> p (s i)").rearrange("p (o x) -> p o x", o=1).broadcast_to([P, MB, MB * HD]).rearrange("p t (s i) -> p t s i", s=MB),
                                       KQ[:, s, b].rearrange("p (t s o) -> p t s o", t=MB, o=1)
                                       .broadcast_to([P, MB, MB, HD]), ALU.mult).then_inc(o_in_ready, 1)

            def window(w, s, last=False):
                for q in range(4):
                    quarter(w, s, q)
                    if not last:
                        if q == 0:
                            norms(w + 1, 1 - s)
                        if q == 2:
                            pairs(w + 1, 1 - s)

            norms(0, 0)
            pairs(0, 0)
            window(0, 0)
            window(1, 1)
            with pool.Fori(1, NWIN // 2 - 1) as p:
                for s in range(2):
                    window(p * 2 + s, s)
            window(NWIN - 2, 0)
            window(NWIN - 1, 1, last=True)

        @block.vector
        def _(v):
            def squares(w, s):
                v.wait_ge(sq_ready, w + 2)
                v.tensor_reduce(ss[:], sq[:].rearrange("p j t -> p t j"), AX.X, ALU.add).then_inc(chain, 1)
                v.wait_ge(chain, w * CH + 3)
                v.tensor_scalar(ss[:], ss[:], NORM_EPS ** 2, None, ALU.max).then_inc(ss_ready, 1)

            def normalize(w, s):
                v.wait_ge(inv_ready, w + 2)
                v.tensor_tensor(lanes[:, s, k_], lanes[:, s, k_], mid(inv[:], HD), ALU.mult).then_inc(k_ready, 1)

            def solve(w, s):
                def link(ins):
                    ins.then_inc(chain, 1)
                    count[0] += 1
                    v.wait_ge(chain, w * CH + (count[0] + 2))

                count = [1]
                v.wait_ge(g_ready, w + 2)
                if not isinstance(w, int) or w:
                    v.wait_ge(KQ_ready, w * MB + 1)
                v.tensor_reduce(H[:], hprod[:].rearrange("p c j n -> p c n j"), AX.X, ALU.add).then_inc(H_ready, 1)
                link(v.tensor_reduce(G[:], gprod[:].rearrange("p c j n -> p c n j"), AX.X, ALU.add, negate=True))
                v.wait_ge(beta_ready, w + 2)

                def g(lag):
                    at = first_pair(lag, False)
                    return G[:, at:at + MB - lag, :].rearrange("p c n -> p n c").rearrange("p n (o c) -> p o n c", o=1) \
                        .broadcast_to([P, HD, NB, MB - lag])

                one = lambda ap: ap.rearrange("p i (n o) -> p i n o", o=1)
                x = lambda a, b: X[:, :, :, a * MB + b:a * MB + b + 1]
                link(v.tensor_tensor(lag_of(X, 1), steps(s, b_, 1, MB), g(1), ALU.mult))
                link(v.tensor_tensor(N2[:], steps(s, b_, 2, MB), g(2), ALU.mult))
                link(v.tensor_tensor(one(N3[:]), steps(s, b_, 3, MB), g(3), ALU.mult))
                link(v.tensor_tensor(T2[:], lag_of(X, 1)[..., 1:3], lag_of(X, 1)[..., 0:2], ALU.mult))
                link(v.tensor_tensor(lag_of(X, 2), N2[:], T2[:], ALU.add))
                link(v.tensor_tensor(one(T3[:]), N2[:, :, :, 1:2], x(1, 0), ALU.mult))
                link(v.tensor_tensor(N3[:], N3[:], T3[:], ALU.add))
                link(v.tensor_tensor(one(T3[:]), x(3, 2), x(2, 0), ALU.mult))
                v.tensor_tensor(x(3, 0), one(N3[:]), one(T3[:]), ALU.add).then_inc(x_ready, 1)
                v.wait_ge(x_ready, w + 2)
                assert count[0] < CH
                for _ in range(CH - count[0] - 0):
                    v.nop().then_inc(chain, 1)

            def blocks(w, s, q):
                for i in range(QB):
                    b = q * QB + i
                    n = w * NB + b
                    at = slice(b * MB, (b + 1) * MB)
                    key = lanes[:, s, k_, :, at].rearrange("p j (t o) -> p t o j", o=1).broadcast_to([P, MB, HI, HD])
                    half = [slice(h * HI, (h + 1) * HI) for h in range(2)]
                    vt = [lanes[:, s, v_, half[h], at].rearrange("p i t -> p t i") for h in range(2)]
                    bt = [lanes[:, s, b_, half[h], at].rearrange("p i t -> p t i") for h in range(2)]
                    def retrieve(h, at):
                        v.wait_ge(S_ready, n * 2 + (h + 2))
                        v.tensor_tensor(prod[:, h], S[h][:, 0:HI * HD].rearrange("p (o x) -> p o x", o=1).broadcast_to([P, MB, HI * HD]).rearrange("p t (i j) -> p t i j", j=HD),
                                        key, ALU.mult).then_inc(step[h], 1)

                    def reduce(h, at):
                        v.wait_ge(step[h], at)
                        v.tensor_reduce(ret[:, h], prod[:, h], AX.X, ALU.add).then_inc(step[h], 1)

                    def differ(h, at):
                        v.wait_ge(step[h], at)
                        v.tensor_tensor(diff[:, h], vt[h], ret[:, h], ALU.subtract).then_inc(step[h], 1)

                    def weigh(h, at):
                        v.wait_ge(step[h], at)
                        v.tensor_tensor(bd[:, h], bt[h], diff[:, h], ALU.mult).then_inc(step[h], 1)

                    def apply_x(h, at):
                        v.wait_ge(step[h], at)
                        v.tensor_tensor(xprod[:, h],
                                        X[:, half[h], b, :].rearrange("p i (a b) -> p a i b", b=MB),
                                        bd[:, h].rearrange("p b i -> p (b i)").rearrange("p (o x) -> p o x", o=1).broadcast_to([P, MB, MB * HI]).rearrange("p a (b i) -> p a i b", b=MB),
                                        ALU.mult).then_inc(step[h], 1)

                    def sum_x(h, at):
                        v.wait_ge(step[h], at)
                        if h == 0 and (not isinstance(n, int) or n >= R):
                            v.wait_ge(o_in_ready, n - R + 2)
                        v.tensor_reduce(U[:, b % R, :, half[h]], xprod[:, h], AX.X, ALU.add).then_inc(u_ready, 1)

                    def expand(h, at):
                        v.wait_ge(u_ready, n * 2 + (h + 2))
                        v.tensor_tensor(outer[:, h], U[:, b % R, :, half[h]].rearrange("p t (i o) -> p t i o", o=1)
                                        .broadcast_to([P, MB, HI, HD]), key, ALU.mult).then_inc(outer_ready[h], 1)

                    names = dict(P=retrieve, R=reduce, D=differ, B=weigh, X=apply_x, U=sum_x, O=expand)
                    order = "P0 R0 P1 D0 B0 R1 X0 D1 U0 B1 O0 X1 U1 O1"
                    for word in order.split():
                        k = "PRDBXUO".index(word[0])
                        names[word[0]](int(word[1]), n * (OPS - 1) + (k + 1))

            def window(w, s, last=False):
                blocks(w, s, 0)
                if not last:
                    squares(w + 1, 1 - s)
                blocks(w, s, 1)
                if not last:
                    normalize(w + 1, 1 - s)
                blocks(w, s, 2)
                blocks(w, s, 3)
                if not last:
                    solve(w + 1, 1 - s)

            v.memset(X[:], 0.0).then_inc(x_ready, 1)
            v.wait_ge(x_ready, 2)
            v.memset(lag_of(X, 0), 1.0).then_inc(x_ready, 1)
            squares(0, 0)
            normalize(0, 0)
            solve(0, 0)
            window(0, 0)
            window(1, 1)
            with v.Fori(1, NWIN // 2 - 1) as p:
                for s in range(2):
                    window(p * 2 + s, s)
            window(NWIN - 2, 0)
            window(NWIN - 1, 1, last=True)


def attn_out(nc, m, scan_dram, w_out, b_out):
    with ExitStack() as c:
        def sb(name, shape, dt=F32):
            return c.enter_context(nc.sbuf_tensor("ao_" + name, shape, dt))

        sems = []

        def sem(name):
            sems.append(c.enter_context(nc.semaphore("ao_" + name)))
            return sems[-1]

        W, brow, ones = sb("w_out_sb", [P, KC, D]), sb("brow", [1, D]), sb("ones", [1, P])
        oT, eps = sb("oT", [P, 2, KC, GN]), sb("eps", [P, 1])
        ps = [c.enter_context(nc.psum_tensor(f"ao_ps{k}", [P, 512], F32)) for k in range(4)]
        w_in, x_scaled, y_ready, stat, chain, need_sqrt, have_sqrt, consts = map(sem, (
            "w_in", "x_scaled", "y_ready", "stat", "chain", "need_sqrt", "have_sqrt", "consts"))
        o_in = [sem("o_in0"), sem("o_in1")]
        prime(nc, sems)
        block = c.enter_context(nc.Block())

        @block.sync
        def _(sp):
            sp.dma_start(W[:], w_out.rearrange("(k p) f -> p k f", p=P)).then_inc(w_in, 16)
            sp.dma_start(brow[:], b_out.rearrange("(o f) -> o f", o=1)).then_inc(w_in, 16)
            with sp.Fori(0, B) as b:
                for s in range(2):
                    sp.wait_ge(y_ready, b * 8 + 1)
                    sp.dma_start(oT[:, s], scan_dram[bass.ds(b, 1), :, s * GN:(s + 1) * GN]
                                 .rearrange("o (c p) t -> p (o c) t", p=P)).then_inc(o_in[s], 16)

        @block.tensor
        def _(pe):
            pe.wait_ge(w_in, 33)
            pe.wait_ge(consts, 3)
            with pe.Fori(0, B) as b:
                for s in range(2):
                    pe.wait_ge(o_in[s], b * 16 + 16 + 1)
                    for r in range(GT):
                        pe.wait_ge(stat, b * 8 + 4 * s + 1)
                        pe.matmul(ps[r][:, 0:D], ones[:], brow[:], start=True, stop=False)
                        for k in range(KC):
                            last = pe.matmul(ps[r][:, 0:D], oT[:, s, k, r * P:(r + 1) * P], W[:, k, :],
                                             start=False, stop=k == KC - 1)
                        last.then_inc(y_ready, 1)

        @block.scalar
        def _(act):
            with act.Fori(0, B) as b:
                for r in range(BT):
                    n = b * BT + r
                    xt = m["x"][:, bass.ds(n, 1), :].rearrange("p o d -> p (o d)")
                    act.activation(xt, xt, ACT.Identity, bias=m["shift1"][:, bass.ds(n, 1)],
                                   scale=m["rs1"][:, bass.ds(n, 1)]).then_inc(x_scaled, 1)
            act.wait_ge(need_sqrt, 2)
            act.activation(m["r1"][:], m["var"][:], ACT.Sqrt, bias=eps[:]).then_inc(have_sqrt, 1)

        @block.vector
        def _(v):
            link = Chain(v, chain)
            v.memset(ones[:], 1.0).then_inc(consts, 1)
            v.memset(eps[:], EPS).then_inc(consts, 1)
            with v.Fori(0, B) as b:
                for r in range(BT):
                    n = b * BT + r
                    xt = m["x"][:, bass.ds(n, 1), :].rearrange("p o d -> p (o d)")
                    v.wait_ge(x_scaled, n + 1 + 1)
                    v.wait_ge(y_ready, n + 1 + 1)
                    v.tensor_tensor(xt, xt, ps[r % GT][:, 0:D], ALU.add).then_inc(chain, 1)
                    v.wait_ge(chain, n + 1 + 1)
                    v.bn_stats(m["stats"][:, bass.ds(n, 1), :].rearrange("p o s -> p (o s)"), xt).then_inc(stat, 1)
            v.wait_ge(stat, TILES + 1)
            link.base = TILES
            row_moments(v, link, m)
            v.nop().then_inc(need_sqrt, 1)
            v.wait_ge(have_sqrt, 2)
            link(v.reciprocal(m["r1"][:], m["r1"][:]))
            link(v.scalar_tensor_tensor(m["shift1"][:], m["mu"][:], -1.0, m["r1"][:], ALU.mult, ALU.mult))


def route(nc, m, router_w, ws_gate_up, ws_down, rows_dram, counts_dram, ends_dram, out):
    with ExitStack() as c:
        def sb(name, shape, dt=F32):
            return c.enter_context(nc.sbuf_tensor("rt_" + name, shape, dt))

        sems = []

        def sem(name):
            sems.append(c.enter_context(nc.semaphore("rt_" + name)))
            return sems[-1]

        RW, RT = sb("router_rows", [E, D]), sb("router_T", [P, KC, E])
        GU, DN = sb("shared_gu", [P, KC, 2 * F]), sb("shared_dn", [FH, 2, D])
        rows, hT = sb("rows", [P, 2, GT, ROW]), sb("hT", [P, 2, KC, GN])
        neg, m8, e8 = sb("neg", [P, GT]), sb("m8", [P, GT, TOPK]), sb("e8", [P, GT, TOPK])
        ex, rep, mask = sb("ex", [P, GT, E]), sb("rep", [P, GT, E]), sb("mask", [P, GT, E], BF16)
        tri, trif = sb("tri", [P, P + 1], BF16), sb("trif", [P, P + 1])
        cnt, tot = sb("cnt", [E, 2, GT, P]), sb("tot", [E, TILES])
        wsum, carrier = sb("wsum", [P, GT]), sb("carrier", [P, 1])
        th, act_in = sb("th", [FH, 2, GN]), sb("act_in", [FH, 2, GN])
        zero, onesE = sb("zero", [P, ROW]), sb("onesE", [E, TILES])
        tp = [c.enter_context(nc.psum_tensor(f"rt_tp{k}", [P, GN], F32)) for k in range(KC)]
        lg = c.enter_context(nc.psum_tensor("rt_lg", [P, GT, P], F32))
        cp = c.enter_context(nc.psum_tensor("rt_cp", [E, 2, 512], F32))
        gu = [c.enter_context(nc.psum_tensor(f"rt_gu{k}", [P, GN], F32)) for k in range(3)]
        names = ("w_in consts h_ready tp_ready hT_ready lg_ready mx ex_ready topk mask_ready cp_ready cnt_ready "
                 "gate_ready up_ready th_ready t_done a_done dn_ready x_done chain tail_sem id0 rt0 group_chain").split()
        q = {n: sem(n) for n in names}
        rows_out, cnt_out, base_out = ([sem(f"{n}{s}") for s in range(2)] for n in ("rows_out", "cnt_out", "base_out"))
        prime(nc, sems)
        block = c.enter_context(nc.Block())
        groups = 2 * B

        @block.sync
        def _(sp):
            sp.dma_start(RW[:], router_w).then_inc(q["w_in"], 16)
            sp.dma_start(GU[:], ws_gate_up.rearrange("(k p) f -> p k f", p=P)).then_inc(q["w_in"], 16)
            sp.dma_start(DN[:], ws_down.rearrange("(k p) f -> p k f", p=FH)).then_inc(q["w_in"], 16)
            sp.wait_ge(q["consts"], 2)
            sp.dma_start(rows_dram[NT:NT + P, :], zero[:]).then_inc(q["tail_sem"], 16)
            sp.dma_start(out[NT:NT + P, :], zero[:, 0:D]).then_inc(q["tail_sem"], 16)
            with sp.Fori(0, B) as b:
                for s in range(2):
                    g = b * 2 + s
                    sp.wait_ge(q["mask_ready"], g + 1 + 1)
                    sp.dma_start(rows_dram.rearrange("(n p) f -> p n f", p=P)[:, bass.ds(g * GT, GT), :],
                                 rows[:, s]).then_inc(rows_out[s], 16)
                    sp.wait_ge(q["cnt_ready"], g + 1 + 1)
                    sp.dma_start(counts_dram.rearrange("(e n) t -> e n t", e=E)[:, bass.ds(g * GT, GT), :],
                                 cnt[:, s]).then_inc(cnt_out[s], 16)
                    sp.wait_ge(q["x_done"], g * GT + GT + 1)
                    sp.dma_start(out.rearrange("(n p) f -> p n f", p=P)[:, bass.ds(g * GT, GT), :],
                                 m["x"][:, bass.ds(g * GT, GT), :]).then_inc(base_out[s], 16)
            sp.wait_ge(q["chain"], 2)
            sp.dma_start(ends_dram.rearrange("o (e n) -> (o e) n", e=E), tot[:]).then_inc(q["tail_sem"], 16)
            sp.wait_ge(q["tail_sem"], 49)
            for s in range(2):
                for x in (rows_out, cnt_out, base_out):
                    sp.wait_ge(x[s], 16 * B + 1)

        @block.gpsimd
        def _(pool):
            pool.memset(zero[:], 0.0).then_inc(q["consts"], 1)
            pool.memset(onesE[:], 1.0).then_inc(q["consts"], 1)
            pool.memset(trif[:], 2.0).then_inc(q["id0"], 1)
            pool.wait_ge(q["id0"], 2)
            pool.affine_select(out=trif[:, 0:P], in_=trif[:, 0:P], compare_op=ALU.is_ge, fill=0.0, base=0,
                               pattern=[[1, P]], channel_multiplier=-1).then_inc(q["id0"], 1)
            pool.wait_ge(q["id0"], 3)
            pool.tensor_tensor(trif[:, 0:P], trif[:, 0:P], m["ident"][:], ALU.subtract).then_inc(q["id0"], 1)
            pool.wait_ge(q["id0"], 4)
            pool.tensor_copy(tri[:], trif[:]).then_inc(q["consts"], 1)

        @block.tensor
        def _(pe):
            pe.wait_ge(q["w_in"], 49)
            for k in range(KC):
                last = pe.transpose(tp[k][:, 0:E], RW[:, k * P:(k + 1) * P], m["ident"][0:E, 0:E])
            last.then_inc(q["rt0"], 1)
            pe.wait_ge(q["rt0"], 4)
            pe.wait_ge(q["consts"], 4)
            with pe.Fori(0, B) as b:
                for s in range(2):
                    g = b * 2 + s
                    pe.wait_ge(q["hT_ready"], g * 2 + 1)
                    pe.wait_ge(q["h_ready"], g * GT + GT + 1)
                    for r in range(GT):
                        for k in range(KC):
                            last = pe.transpose(tp[k][:, r * P:(r + 1) * P], rows[:, s, r, k * P:(k + 1) * P],
                                                m["ident"][:])
                    last.then_inc(q["tp_ready"], 1)
                    pe.wait_ge(q["hT_ready"], g * 2 + 2 + 1)
                    pe.wait_ge(q["ex_ready"], g * GT + 1)
                    for r in range(GT):
                        for k in range(KC):
                            last = pe.matmul(lg[:, r, 0:E], hT[:, s, k, r * P:(r + 1) * P], RT[:, k, :],
                                             start=k == 0, stop=k == KC - 1)
                    last.then_inc(q["lg_ready"], 1)
                    for f in range(2):
                        pe.wait_ge(q["t_done"], g * 2 + f + 1)
                        for j in range(KC):
                            last = pe.matmul(gu[0][0:FH, :], GU[:, j, f * FH:(f + 1) * FH], hT[:, s, j, :],
                                             start=j == 0, stop=j == KC - 1)
                        last.then_inc(q["gate_ready"], 1)
                        pe.wait_ge(q["a_done"], g * 2 + f + 1)
                        for j in range(KC):
                            last = pe.matmul(gu[1][0:FH, :], GU[:, j, F + f * FH:F + (f + 1) * FH], hT[:, s, j, :],
                                             start=j == 0, stop=j == KC - 1)
                        last.then_inc(q["up_ready"], 1)
                    pe.wait_ge(q["mask_ready"], g + 1 + 1)
                    pe.wait_ge(q["cnt_ready"], g + 1)
                    for r in range(GT):
                        last = pe.matmul(cp[:, r // 2, (r % 2) * 256:(r % 2) * 256 + P + 1], mask[:, r, :], tri[:],
                                         start=True, stop=True)
                    last.then_inc(q["cp_ready"], 1)
                    pe.wait_ge(q["a_done"], g * 2 + 2 + 1)
                    for r in range(GT):
                        h = r % 2
                        pe.wait_ge(q["x_done"], g * GT + r + 1)
                        for f in range(2):
                            last = pe.matmul(gu[2][:, 0:D], act_in[:, f, r * P:(r + 1) * P], DN[:, f, :],
                                             start=f == 0, stop=f == 1)
                        last.then_inc(q["dn_ready"], 1)

        @block.scalar
        def _(act):
            act.wait_ge(q["rt0"], 2)
            for k in range(KC):
                act.copy(RT[:, k, :], tp[k][:, 0:E]).then_inc(q["rt0"], 1)
            with act.Fori(0, B) as b:
                for s in range(2):
                    g = b * 2 + s
                    act.wait_ge(rows_out[s], b * 16 + 1)
                    for r in range(GT):
                        n = b * BT + (s * GT + r)
                        act.activation(rows[:, s, r, 0:D], m["x"][:, bass.ds(n, 1), :].rearrange("p o d -> p (o d)"),
                                       ACT.Identity, bias=m["shift1"][:, bass.ds(n, 1)], scale=m["r1"][:, bass.ds(n, 1)]
                                       ).then_inc(q["h_ready"], 1)
                    act.wait_ge(q["tp_ready"], g + 1 + 1)
                    for k in range(KC):
                        act.copy(hT[:, s, k, :], tp[k][:]).then_inc(q["hT_ready"], 1)
                    for r in range(GT):
                        act.wait_ge(q["mx"], g * GT + GT + 1)
                        act.activation(ex[:, r, :], lg[:, r, 0:E], ACT.Exp, bias=neg[:, r:r + 1]
                                       ).then_inc(q["ex_ready"], 1)
                    for f in range(2):
                        act.wait_ge(q["gate_ready"], g * 2 + (f + 1) + 1)
                        act.wait_ge(q["t_done"], g * 2 + 1)
                        act.activation(th[:, f, :], gu[0][0:FH, :], ACT.Tanh, scale=0.5).then_inc(q["th_ready"], 1)
                    act.wait_ge(q["cp_ready"], g + 1 + 1)
                    act.wait_ge(cnt_out[s], b * 16 + 1)
                    act.copy(tot[:, bass.ds(g * GT, GT)].rearrange("e (a r) -> e a r", r=2),
                             cp[:].rearrange("e a (r t) -> e a r t", r=2)[:, :, :, P]).then_inc(q["topk"], 1)
                    act.copy(cnt[:, s].rearrange("e (a r) t -> e a r t", r=2),
                             cp[:].rearrange("e a (r t) -> e a r t", r=2)[:, :, :, 0:P]).then_inc(q["cnt_ready"], 1)

        @block.vector
        def _(v):
            L = 9
            cs = q["group_chain"]
            with v.Fori(0, B) as b:
                for s in range(2):
                    g = b * 2 + s
                    link2 = Chain(v, cs, g * L)
                    v.wait_ge(q["lg_ready"], g + 1 + 1)
                    v.memset(carrier[:], 0.0)
                    for r in range(GT):
                        last = v.max(m8[:, r, :], lg[:, r, 0:E])
                    link2(last)
                    v.wait_ge(q["ex_ready"], g * GT + 1)
                    link2(v.tensor_scalar(neg[:], m8[:, :, 0], -1.0, None, ALU.mult))
                    v.nop().then_inc(q["mx"], GT)
                    v.wait_ge(q["ex_ready"], g * GT + GT + 1)
                    v.memset(carrier[:], 0.0)
                    for r in range(GT):
                        last = v.max(e8[:, r, :], ex[:, r, :])
                    link2(last)
                    link2(v.tensor_reduce(wsum[:], e8[:], AX.X, ALU.add))
                    link2(v.reciprocal(wsum[:], wsum[:]))
                    v.memset(carrier[:], 0.0)
                    for r in range(GT):
                        last = v.match_replace(rep[:, r, :], e8[:, r, :], ex[:, r, :], -1.0)
                    link2(last)
                    v.wait_ge(q["cp_ready"], g + 1)
                    link2(v.tensor_scalar(mask[:], rep[:], 0.0, None, ALU.is_lt))
                    link2(v.tensor_tensor(ex[:], ex[:], mask[:], ALU.mult))
                    link2(v.tensor_tensor(rows[:, s, :, D:ROW], ex[:],
                                          wsum[:].rearrange("p (r o) -> p r o", o=1).broadcast_to([P, GT, E]), ALU.mult))
                    v.nop().then_inc(q["mask_ready"], 1)
                    for f in range(2):
                        v.wait_ge(q["th_ready"], g * 2 + (f + 1) + 1)
                        v.scalar_tensor_tensor(th[:, f, :], th[:, f, :], 1.0, gu[0][0:FH, :], ALU.add, ALU.mult
                                               ).then_inc(q["t_done"], 1)
                        v.wait_ge(q["t_done"], g * 2 + (f + 1) + 1)
                        v.wait_ge(q["up_ready"], g * 2 + (f + 1) + 1)
                        v.wait_ge(q["dn_ready"], g * GT + 1)
                        v.scalar_tensor_tensor(act_in[:, f, :], th[:, f, :], 0.5, gu[1][0:FH, :], ALU.mult, ALU.mult
                                               ).then_inc(q["a_done"], 1)
                    for r in range(GT):
                        n = b * BT + (s * GT + r)
                        xt = m["x"][:, bass.ds(n, 1), :].rearrange("p o d -> p (o d)")
                        v.wait_ge(q["dn_ready"], n + 1 + 1)
                        v.tensor_tensor(xt, xt, gu[2][:, 0:D], ALU.add).then_inc(q["x_done"], 1)
            v.wait_ge(q["topk"], groups + 1)
            v.wait_ge(q["consts"], 3)
            v.tensor_scalar(tot[:], tot[:], 0.5, None, ALU.mult).then_inc(cs, 1)
            v.wait_ge(cs, groups * L + 1 + 1)
            v.tensor_tensor_scan(tot[:], onesE[:], tot[:], 0.0, ALU.mult, ALU.add).then_inc(q["chain"], 1)


def experts(nc, w_gate, w_up, w_down, rows_dram, counts_dram, ends_dram, out):
    R = 4
    with ExitStack() as c:
        def sb(name, shape, dt=F32):
            return c.enter_context(nc.sbuf_tensor("ex_" + name, shape, dt))

        sems = []

        def sem(name):
            sems.append(c.enter_context(nc.semaphore("ex_" + name)))
            return sems[-1]

        ident = sb("ident2", [P, P])
        ends, le = sb("ends", [P, E, TILES]), sb("le", [P, E, TILES])
        carrier, zero = sb("carrier", [P, 3 * R + 1]), sb("zero", [P, 1])
        slot, tok = sb("slot", [P, 1]), sb("tok", [P, P])
        tile_of, first, none, goal = sb("tile_of", [P, E]), sb("first", [P, E]), sb("none", [P, E]), sb("goal", [P, E])
        row_f, base = sb("row_f", [P, E]), sb("base", [P, E])
        row_id, tok_id = sb("row_id", [P, E], U32), sb("tok_id", [P, E], U32)
        eoff = sb("eoff", [P, E])
        row_cur, tok_cur = sb("row_cur", [P, R], U32), sb("tok_cur", [P, R], U32)
        vr, junk, pos = sb("vr", [P, R, P]), sb("junk", [P, R, P]), sb("pos", [P, R])
        WGU, WD = sb("wgu", [P, R, 2, KC, F]), sb("wd", [FH, R, 2, D])
        xg, xT = sb("xg", [P, R, ROW]), sb("xT", [P, 2, KC, P])
        th, t2, aT, yw = sb("th", [FH, 2, 2, P]), sb("t2", [FH, 2, 2, P]), sb("aT", [FH, 2, 2, P]), sb("yw", [P, R, D])
        tp = [c.enter_context(nc.psum_tensor(f"ex_tp{k}", [P, 512], F32)) for k in range(2)]
        gu = [c.enter_context(nc.psum_tensor(f"ex_gu{k}", [P, 4, P], F32)) for k in range(2)]
        yp = [c.enter_context(nc.psum_tensor(f"ex_yp{k}", [P, 512], F32)) for k in range(2)]
        names = ("ends_in consts chain ids row_copied pos_done pos_copied tok_copied tp_ready xT_ready gu_ready "
                 "th_ready t2_ready a_ready y_ready yw_ready id0 carried").split()
        q = {n: sem(n) for n in names}
        w_in, v_in, x_in, added = ([sem(f"{n}{s}") for s in range(R)] for n in ("w_in", "v_in", "x_in", "added"))
        prime(nc, sems[:len(names)])
        block = c.enter_context(nc.Block())

        @block.sync
        def _(sp):
            sp.dma_start(ends[:].rearrange("p e n -> p (e n)"), ends_dram.broadcast_to([P, E * TILES])).then_inc(q["ends_in"], 16)
            with sp.Fori(0, E // R) as it:
                for s in range(R):
                    e = it * R + s
                    sp.wait_ge(q["y_ready"], it * R + 1)
                    for g, w in enumerate((w_gate, w_up)):
                        sp.dma_start(WGU[:, s, g], w[bass.ds(e, 1)].rearrange("o (k p) f -> p (o k) f", p=P)
                                     ).then_inc(w_in[s], 16)
                    sp.dma_start(WD[:, s], w_down[bass.ds(e, 1)].rearrange("o (k p) f -> p (o k) f", p=FH)
                                 ).then_inc(w_in[s], 16)

        @block.gpsimd
        def _(pool):
            def carry(at):
                pool.tensor_tensor(carrier[:, at:at + 1], zero[:], zero[:], ALU.add).then_inc(q["carried"], 1)

            pool.memset(zero[:], 0.0).then_inc(q["consts"], 1)
            pool.wait_ge(q["consts"], 2)
            pool.memset(ident[:], 0.0).then_inc(q["id0"], 1)
            pool.wait_ge(q["id0"], 2)
            pool.affine_select(out=ident[:], in_=ident[:], compare_op=ALU.not_equal, fill=1.0,
                               base=0, pattern=[[-1, P]], channel_multiplier=1).then_inc(q["consts"], 1)
            pool.iota(slot[:], pattern=[[0, 1]], base=0, channel_multiplier=1,
                      allow_small_or_imprecise_dtypes=True).then_inc(q["consts"], 1)
            pool.iota(tok[:], pattern=[[1, P]], base=0, channel_multiplier=0,
                      allow_small_or_imprecise_dtypes=True).then_inc(q["consts"], 1)
            pool.iota(eoff[:], pattern=[[TILES, E]], base=0, channel_multiplier=0,
                      allow_small_or_imprecise_dtypes=True).then_inc(q["consts"], 1)
            with pool.Fori(0, E // R) as it:
                for s in range(R):
                    pool.wait_ge(q["row_copied"], it * R + (s + 1) + 1)
                    pool.wait_ge(q["pos_done"], it * R + 1)
                    carry(s)
                    pool.indirect_dma_start(
                        out=vr[:, s], out_offset=None, in_=counts_dram,
                        in_offset=bass.IndirectOffsetOnAxis(ap=row_cur[:, s:s + 1], axis=0),
                        bounds_check=E * TILES - 1).then_inc(v_in[s], 16)
            with pool.Fori(0, E // R) as it:
                for s in range(R):
                    pool.wait_ge(q["tok_copied"], it * R + (s + 1) + 1)
                    pool.wait_ge(q["yw_ready"], it * R + 1)
                    carry(R + s)
                    pool.indirect_dma_start(
                        out=xg[:, s], out_offset=None, in_=rows_dram,
                        in_offset=bass.IndirectOffsetOnAxis(ap=tok_cur[:, s:s + 1], axis=0),
                        bounds_check=NT + P - 1).then_inc(x_in[s], 16)
                for s in range(R):
                    pool.wait_ge(q["yw_ready"], it * R + (s + 1) + 1)
                    if s:
                        pool.wait_ge(added[s - 1], it * 16 + 16)
                    carry(2 * R + s)
                    pool.indirect_dma_start(
                        out=out, out_offset=bass.IndirectOffsetOnAxis(ap=tok_cur[:, s:s + 1], axis=0),
                        in_=yw[:, s], in_offset=None, bounds_check=NT + P - 1, compute_op=ALU.add
                    ).then_inc(added[s], 16)
                pool.wait_ge(added[R - 1], it * 16 + 16)
                carry(3 * R)
            pool.wait_ge(added[R - 1], 16 * (E // R))

        @block.tensor
        def _(pe):
            pe.wait_ge(q["consts"], 3)
            with pe.Fori(0, E // R) as it:
                for s in range(R):
                    d = s % 2
                    e = it * R + s
                    pe.wait_ge(x_in[s], it * 16 + 16)
                    if s >= 2:
                        pe.wait_ge(q["xT_ready"], e - 1 + 1)
                    else:
                        pe.wait_ge(q["xT_ready"], it * R + 1)
                    for k in range(KC):
                        last = pe.transpose(tp[d][:, k * P:(k + 1) * P], xg[:, s, k * P:(k + 1) * P], ident[:])
                    last.then_inc(q["tp_ready"], 1)
                    pe.wait_ge(w_in[s], it * 48 + 48)
                    pe.wait_ge(q["xT_ready"], e + 1 + 1)
                    pe.wait_ge(q["a_ready"], (e - 1 if s >= 2 else it * R) + 1)
                    for g in range(2):
                        for f in range(2):
                            for k in range(KC):
                                last = pe.matmul(gu[d][0:FH, g * 2 + f, :], WGU[:, s, g, k, f * FH:(f + 1) * FH],
                                                 xT[:, d, k, :], start=k == 0, stop=k == KC - 1)
                    last.then_inc(q["gu_ready"], 1)
                    pe.wait_ge(q["a_ready"], e + 1 + 1)
                    pe.wait_ge(q["yw_ready"], (e - 1 if s >= 2 else it * R) + 1)
                    for f in range(2):
                        last = pe.matmul(yp[d][:, 0:D], aT[:, d, f, :], WD[:, s, f, :], start=f == 0, stop=f == 1)
                    last.then_inc(q["y_ready"], 1)

        @block.scalar
        def _(act):
            with act.Fori(0, E // R) as it:
                for s in range(R):
                    d = s % 2
                    e = it * R + s
                    act.wait_ge(q["tp_ready"], e + 1 + 1)
                    act.wait_ge(q["gu_ready"], (e - 1 if s >= 2 else it * R) + 1)
                    act.copy(xT[:, d].rearrange("p k t -> p (k t)"), tp[d][:, 0:KC * P]).then_inc(q["xT_ready"], 1)
                    act.wait_ge(q["gu_ready"], e + 1 + 1)
                    act.wait_ge(q["t2_ready"], (e - 1 if s >= 2 else it * R) + 1)
                    act.activation(th[:, d], gu[d][0:FH, 0:2, :], ACT.Tanh, scale=0.5).then_inc(q["th_ready"], 1)
                    act.wait_ge(q["y_ready"], e + 1 + 1)
                    act.wait_ge(q["carried"], it * (2 * R + 1) + E + 1)
                    act.activation(yw[:, s], yp[d][:, 0:D], ACT.Copy, scale=xg[:, s, bass.ds(e + D, 1)]
                                   ).then_inc(q["yw_ready"], 1)

        @block.vector
        def _(v):
            link = Chain(v, q["chain"])
            v.wait_ge(q["ends_in"], 17)
            v.wait_ge(q["consts"], 6)
            sc = slot[:, 0:1]
            link(v.tensor_scalar(le[:], ends[:], sc, None, ALU.is_le))
            link(v.tensor_reduce(tile_of[:], le[:], AX.X, ALU.add))
            link(v.tensor_tensor(le[:], le[:], ends[:], ALU.mult))
            link(v.tensor_reduce(first[:], le[:], AX.X, ALU.max))
            link(v.tensor_scalar(none[:], tile_of[:], float(TILES), None, ALU.is_ge))
            link(v.tensor_scalar(goal[:], first[:], sc, -2.0, ALU.subtract, ALU.mult))
            link(v.tensor_scalar(goal[:], goal[:], 1.0, None, ALU.add))
            link(v.scalar_tensor_tensor(goal[:], none[:], -4.0 * NT, goal[:], ALU.mult, ALU.add))
            link(v.tensor_scalar(row_f[:], tile_of[:], float(TILES - 1), None, ALU.min))
            link(v.tensor_tensor(row_f[:], row_f[:], eoff[:], ALU.add))
            link(v.tensor_copy(row_id[:], row_f[:]))
            link(v.tensor_scalar(base[:], none[:], sc, None, ALU.mult))
            link(v.scalar_tensor_tensor(base[:], tile_of[:], float(P), base[:], ALU.mult, ALU.add))
            with v.Fori(0, E // R) as it:
                for s in range(R):
                    v.wait_ge(q["carried"], it * R + 1)
                    v.tensor_copy(row_cur[:, s:s + 1], row_id[:, bass.ds(it * R + s, 1)]).then_inc(q["row_copied"], 1)
                for s in range(R):
                    v.wait_ge(v_in[s], it * 16 + 16)
                    v.scalar_tensor_tensor(junk[:, s], vr[:, s], goal[:, bass.ds(it * R + s, 1)], tok[:], ALU.is_equal,
                                           ALU.mult, accum_out=pos[:, s:s + 1]).then_inc(q["pos_done"], 1)
                    v.wait_ge(q["pos_done"], it * R + (s + 1) + 1)
                    v.tensor_tensor(tok_id[:, bass.ds(it * R + s, 1)], pos[:, s:s + 1], base[:, bass.ds(it * R + s, 1)],
                                    ALU.add).then_inc(q["ids"], 1)
            v.wait_ge(q["ids"], E + 1)
            with v.Fori(0, E // R) as it:
                for s in range(R):
                    v.wait_ge(q["carried"], it * (2 * R + 1) + E + 1)
                    v.tensor_copy(tok_cur[:, s:s + 1], tok_id[:, bass.ds(it * R + s, 1)]).then_inc(q["tok_copied"], 1)
                for s in range(R):
                    d = s % 2
                    e = it * R + s
                    v.wait_ge(q["th_ready"], e + 1 + 1)
                    v.scalar_tensor_tensor(t2[:, d], th[:, d], 1.0, gu[d][0:FH, 0:2, :], ALU.add, ALU.mult
                                           ).then_inc(q["t2_ready"], 1)
                    v.wait_ge(q["t2_ready"], e + 1 + 1)
                    v.wait_ge(q["y_ready"], (e - 1 if s >= 2 else it * R) + 1)
                    v.scalar_tensor_tensor(aT[:, d], t2[:, d], 0.5, gu[d][0:FH, 2:4, :], ALU.mult, ALU.mult
                                           ).then_inc(q["a_ready"], 1)


_INS = ['L0_attn_x', 'L0_attn_ln_g', 'L0_attn_ln_b', 'L0_attn_w_qkvb', 'L0_attn_b_qkvb', 'L0_attn_w_out',
        'L0_attn_b_out', 'L0_ffn_router_w', 'L0_ffn_w_gate', 'L0_ffn_w_up', 'L0_ffn_w_down',
        'L0_ffn_ws_gate_up', 'L0_ffn_ws_down']


def kernel(**inputs):
    import numpy as _np
    import concourse.bacc as _bacc
    from concourse import mybir as _mybir
    from concourse.bass_utils import run_bass_kernel_spmd as _run

    nc = _bacc.Bacc("TRN2", target_bir_lowering=False, num_devices=1)
    arrays, args = {}, []
    for name in _INS:
        a = _np.ascontiguousarray(inputs[name])
        arrays[f"in_{name}_dram"] = a
        args.append(nc.dram_tensor(f"in_{name}_dram", a.shape, _mybir.dt.from_np(a.dtype), kind="ExternalInput").ap())
    args.append(nc.dram_tensor("out_0_dram", (NT + P, D), F32, kind="ExternalOutput").ap())
    build(nc, *args)
    r = _run(nc, [arrays], core_ids=[0])
    return r.results[0]["out_0_dram"][0:NT].reshape(B, T, D)
```

```python
import concourse.bass as bass
from concourse import mybir
from contextlib import ExitStack

F32 = mybir.dt.float32
BF16 = mybir.dt.bfloat16
U32 = mybir.dt.uint32
ALU = mybir.AluOpType
ACT = mybir.ActivationFunctionType
AX = mybir.AxisListType

B, T, D = 8, 1024, 256
NH, HD = 16, 16
NT = B * T
P = 128
TILES = NT // P
BT = T // P
KC = D // P
GT = 4
GN = GT * P
PROJ = 4 * D
PC = PROJ // P
E, TOPK, F = 64, 8, 192
FH = F // 2
ROW = D + E
EPS, NORM_EPS = 1e-5, 1e-6
WIN = 64
MB = 4
NWIN = T // WIN


class Chain:

    def __init__(self, eng, sem, base=0, first=1):
        self.eng, self.sem, self.base, self.first, self.n = eng, sem, base, first, 0

    def __call__(self, ins):
        ins.then_inc(self.sem, 1)
        self.n += 1
        self.eng.wait_ge(self.sem, self.base + self.n + self.first)


def mid(ap, count):
    return ap.rearrange("p (o n) -> p o n", o=1).broadcast_to([ap.shape[0], count, ap.shape[1]])


def later(n, first):
    return not isinstance(n, int) or n >= first


def prime(nc, sems, start=1):
    with nc.Block() as block:
        @block.sync
        def _(sp):
            for s in sems:
                sp.nop().then_inc(s, start)


def build(nc, x, ln_g, ln_b, w_qkvb, b_qkvb, w_out, b_out, router_w, w_gate, w_up, w_down, ws_gate_up,
          ws_down, out):
    scratch = [nc.dram_tensor(n, s, F32, kind="Internal").ap() for n, s in (
        ("lanes_dram", (B, PROJ, T)), ("scan_dram", (B, D, T)), ("rows_dram", (NT + P, ROW)),
        ("counts_dram", (E * TILES, P)), ("ends_dram", (1, E * TILES)))]
    lanes_dram, scan_dram, rows_dram, counts_dram, ends_dram = scratch
    with ExitStack() as keep:
        def sb(name, shape, dt=F32):
            return keep.enter_context(nc.sbuf_tensor(name, shape, dt))

        m = {
            "x": sb("x_sb", [P, TILES, D]),
            "ident": sb("ident", [P, P]),
            "mu": sb("mu", [P, TILES]), "var": sb("var", [P, TILES]),
            "stats": sb("stats", [P, TILES, 6]),
            "r1": sb("r1", [P, TILES]), "r12": sb("r12", [P, TILES]), "shift": sb("shift", [P, TILES]),
            "rs1": sb("rs1", [P, TILES]), "shift1": sb("shift1", [P, TILES]),
            "tmp": sb("tmp", [P, TILES]), "tmp2": sb("tmp2", [P, TILES]),
        }
        with ExitStack() as c:
            w, load = projection_weights(nc, c, ln_g, ln_b, w_qkvb, b_qkvb)
            moments(nc, m, x, load)
            project(nc, m, w, lanes_dram)
        scan(nc, m, lanes_dram, scan_dram)
        attn_out(nc, m, scan_dram, w_out, b_out)
        route(nc, m, router_w, ws_gate_up, ws_down, rows_dram, counts_dram, ends_dram, out)
    experts(nc, w_gate, w_up, w_down, rows_dram, counts_dram, ends_dram, out)


def row_moments(v, link, m):
    half = lambda i: m["stats"][:, :, i]
    link(v.tensor_tensor(m["mu"][:], half(1), half(4), ALU.add))
    link(v.tensor_tensor(m["tmp"][:], half(1), half(4), ALU.subtract))
    link(v.tensor_scalar(m["mu"][:], m["mu"][:], 0.5, None, ALU.mult))
    link(v.tensor_scalar(m["tmp"][:], m["tmp"][:], 0.5, None, ALU.mult))
    link(v.tensor_tensor(m["tmp"][:], m["tmp"][:], m["tmp"][:], ALU.mult))
    link(v.tensor_tensor(m["var"][:], half(2), half(5), ALU.add))
    link(v.scalar_tensor_tensor(m["var"][:], m["var"][:], 1.0 / D, m["tmp"][:], ALU.mult, ALU.add))


def moments(nc, m, x, load_projection):
    XQ = 4
    with ExitStack() as c:
        stat, chain, need_sqrt, have_sqrt, id0 = (
            c.enter_context(nc.semaphore("mo_" + n)) for n in ("stat", "chain", "need_sqrt", "have_sqrt", "id0"))
        x_in = [c.enter_context(nc.semaphore(f"mo_x_in{k}")) for k in range(XQ)]
        eps = c.enter_context(nc.sbuf_tensor("mo_eps", [P, 1], F32))
        block = c.enter_context(nc.Block())

        @block.sync
        def _(sp):
            for b in range(B):
                sp.dma_start(m["x"][:, b * BT:(b + 1) * BT, :],
                             x[b].rearrange("(n p) d -> p n d", p=P)).then_inc(x_in[b * XQ // B], 16)
            load_projection(sp)

        @block.gpsimd
        def _(pool):
            pool.memset(m["ident"][:], 0.0).then_inc(id0, 1)
            pool.wait_ge(id0, 1)
            pool.affine_select(out=m["ident"][:], in_=m["ident"][:], compare_op=ALU.not_equal, fill=1.0,
                               base=0, pattern=[[-1, P]], channel_multiplier=1).then_inc(id0, 1)

        @block.scalar
        def _(act):
            act.wait_ge(need_sqrt, 1)
            act.activation(m["r1"][:], m["var"][:], ACT.Sqrt, bias=eps[:]).then_inc(have_sqrt, 1)
            act.wait_ge(need_sqrt, 2)
            act.activation(m["r12"][:], m["tmp"][:], ACT.Sqrt, bias=eps[:]).then_inc(have_sqrt, 1)

        @block.vector
        def _(v):
            link = Chain(v, chain, first=0)
            link(v.memset(eps[:], EPS))
            for k in range(XQ):
                v.wait_ge(x_in[k], 16 * B // XQ)
                with v.Fori(k * B // XQ, (k + 1) * B // XQ) as b:
                    for r in range(BT):
                        n = b * BT + r
                        v.bn_stats(m["stats"][:, bass.ds(n, 1), :].rearrange("p o s -> p (o s)"),
                                   m["x"][:, bass.ds(n, 1), :].rearrange("p o d -> p (o d)")).then_inc(stat, 1)
            v.wait_ge(stat, TILES)
            row_moments(v, link, m)
            v.nop().then_inc(need_sqrt, 1)
            v.wait_ge(have_sqrt, 1)
            link(v.reciprocal(m["r1"][:], m["r1"][:]))
            link(v.tensor_tensor(m["tmp"][:], m["var"][:], m["r1"][:], ALU.mult))
            link(v.tensor_tensor(m["tmp"][:], m["tmp"][:], m["r1"][:], ALU.mult))
            v.nop().then_inc(need_sqrt, 1)
            v.wait_ge(have_sqrt, 2)
            link(v.reciprocal(m["r12"][:], m["r12"][:]))
            link(v.tensor_tensor(m["r12"][:], m["r12"][:], m["r1"][:], ALU.mult))
            link(v.scalar_tensor_tensor(m["shift"][:], m["mu"][:], -1.0, m["r12"][:], ALU.mult, ALU.mult))
            link(v.scalar_tensor_tensor(m["shift1"][:], m["mu"][:], -1.0, m["r1"][:], ALU.mult, ALU.mult))
            link(v.tensor_scalar(m["rs1"][:], m["r1"][:], 1.0, None, ALU.add))


def projection_weights(nc, c, ln_g, ln_b, w_qkvb, b_qkvb):
    w = {n: c.enter_context(nc.sbuf_tensor("pj_" + n, shape, F32)) for n, shape in (
        ("W", [P, KC, PROJ]), ("bias", [P, PC]), ("gain", [P, KC]), ("off", [P, KC]))}
    w["w_in"] = c.enter_context(nc.semaphore("pj_w_in"))
    w["loads"] = 4 * (KC + 2) + 2

    def load(sp):
        for a in range(4):
            for k in range(KC):
                sp.dma_start(w["W"][:, k, :].rearrange("p (h a j) -> p h a j", a=4, j=HD)[:, :, a, :],
                             w_qkvb[k * P:(k + 1) * P, a * D:(a + 1) * D].rearrange("p (h j) -> p h j", j=HD)
                             ).then_inc(w["w_in"], 16)
            for h in range(2):
                row = h * 4 * HD + a * HD
                sp.dma_start(w["bias"][row:row + HD, :],
                             b_qkvb[a * D:(a + 1) * D].rearrange("(c h j) -> h j c", h=2, j=HD)[h],
                             allow_slow_non_contiguous=True).then_inc(w["w_in"], 16)
        for part, vector in (("gain", ln_g), ("off", ln_b)):
            sp.dma_start(w[part][:], vector.rearrange("(c p) -> p c", p=P), allow_slow_non_contiguous=True
                         ).then_inc(w["w_in"], 16)

    return w, load


def project(nc, m, w, lanes_dram):
    with ExitStack() as c:
        def sb(name, shape, dt=F32):
            return c.enter_context(nc.sbuf_tensor("pj_" + name, shape, dt))

        sems = []

        def sem(name):
            sems.append(c.enter_context(nc.semaphore("pj_" + name)))
            return sems[-1]

        W, bias, gain, off = (w[n] for n in ("W", "bias", "gain", "off"))
        xh, nT, stage = sb("xh", [P, GT, D]), sb("nT", [P, 2, KC, GN]), sb("stage", [P, 2, PC, GN])
        tp = [c.enter_context(nc.psum_tensor(f"pj_tp{k}", [P, GN], F32)) for k in range(KC)]
        pj = [c.enter_context(nc.psum_tensor(f"pj_pj{k}", [P, GN], F32)) for k in range(4)]
        xh_ready, tp_ready, nT_ready, pj_ready, dve_out, act_out = map(sem, (
            "xh_ready", "tp_ready", "nT_ready", "pj_ready", "dve_out", "act_out"))
        stored = [sem("stored0"), sem("stored1")]
        prime(nc, sems)
        block = c.enter_context(nc.Block())

        @block.sync
        def _(sp):
            with sp.Fori(0, B) as b:
                for s in range(2):
                    sp.wait_ge(dve_out, b * 8 + 4 * (s + 1) + 1)
                    sp.wait_ge(act_out, b * 8 + 4 * (s + 1) + 1)
                    sp.dma_start(lanes_dram[bass.ds(b, 1), :, s * GN:(s + 1) * GN]
                                 .rearrange("o (c p) t -> p (o c) t", p=P), stage[:, s]).then_inc(stored[s], 16)
            sp.wait_ge(stored[0], 16 * B + 1)
            sp.wait_ge(stored[1], 16 * B + 1)

        @block.vector
        def _(v):
            def normalize(b, s):
                v.wait_ge(tp_ready, b * 2 + s + 1)
                for r in range(GT):
                    n = b * BT + (s * GT + r)
                    v.tensor_scalar(xh[:, r, :], m["x"][:, bass.ds(n, 1), :].rearrange("p o d -> p (o d)"),
                                    m["r12"][:, bass.ds(n, 1)], m["shift"][:, bass.ds(n, 1)],
                                    ALU.mult, ALU.add).then_inc(xh_ready, 1)

            def evacuate(b, s):
                v.wait_ge(stored[s], b * 16 + 1)
                for k in range(4):
                    v.wait_ge(pj_ready, b * 16 + (8 * s + k + 1) + 1)
                    v.tensor_scalar(stage[:, s, k, :], pj[k][:], bias[:, k:k + 1], None,
                                    ALU.add).then_inc(dve_out, 1)

            v.wait_ge(w["w_in"], 16 * w["loads"])
            normalize(0, 0)
            with v.Fori(0, B - 1) as b:
                normalize(b, 1)
                evacuate(b, 0)
                normalize(b + 1, 0)
                evacuate(b, 1)
            normalize(B - 1, 1)
            evacuate(B - 1, 0)
            evacuate(B - 1, 1)

        @block.scalar
        def _(act):
            def copy_nT(b, s):
                act.wait_ge(tp_ready, b * 2 + (s + 1) + 1)
                if later(b, 1):
                    act.wait_ge(pj_ready, b * 16 + (8 * s - 7))
                for k in range(KC):
                    act.activation(nT[:, s, k, :], tp[k][:], ACT.Identity, bias=off[:, k:k + 1],
                                   scale=gain[:, k:k + 1]).then_inc(nT_ready, 1)

            def evacuate(b, s):
                act.wait_ge(stored[s], b * 16 + 1)
                for k in range(4, PC):
                    act.wait_ge(pj_ready, b * 16 + (8 * s + k + 1) + 1)
                    act.activation(stage[:, s, k, :], pj[k % 4][:], ACT.Identity,
                                   bias=bias[:, k:k + 1]).then_inc(act_out, 1)

            act.wait_ge(w["w_in"], 16 * w["loads"])
            copy_nT(0, 0)
            with act.Fori(0, B - 1) as b:
                copy_nT(b, 1)
                evacuate(b, 0)
                copy_nT(b + 1, 0)
                evacuate(b, 1)
            copy_nT(B - 1, 1)
            evacuate(B - 1, 0)
            evacuate(B - 1, 1)

        @block.tensor
        def _(pe):
            def transposes(b, s):
                pe.wait_ge(nT_ready, b * 4 + 2 * s + 1)
                pe.wait_ge(xh_ready, b * 8 + 4 * (s + 1) + 1)
                for r in range(GT):
                    for k in range(KC):
                        last = pe.transpose(tp[k][:, r * P:(r + 1) * P], xh[:, r, k * P:(k + 1) * P],
                                            m["ident"][:])
                last.then_inc(tp_ready, 1)

            def products(b, s):
                pe.wait_ge(nT_ready, b * 4 + 2 * (s + 1) + 1)
                for k in range(PC):
                    if k < 4:
                        pe.wait_ge(act_out, b * 8 + 4 * s + 1)
                    else:
                        pe.wait_ge(dve_out, b * 8 + (4 * s + k - 3) + 1)
                    for j in range(KC):
                        last = pe.matmul(pj[k % 4][:], W[:, j, k * P:(k + 1) * P], nT[:, s, j, :],
                                         start=j == 0, stop=j == KC - 1)
                    last.then_inc(pj_ready, 1)

            pe.wait_ge(w["w_in"], 16 * w["loads"])
            transposes(0, 0)
            with pe.Fori(0, B - 1) as b:
                transposes(b, 1)
                products(b, 0)
                transposes(b + 1, 0)
                products(b, 1)
            transposes(B - 1, 1)
            products(B - 1, 0)
            products(B - 1, 1)


def scan(nc, m, lanes_dram, scan_dram):
    with ExitStack() as c:
        sems = []

        def sb(name, shape, dt=F32):
            return c.enter_context(nc.sbuf_tensor("sc_" + name, shape, dt))

        def pb(name, shape):
            return c.enter_context(nc.psum_tensor("sc_" + name, shape, F32))

        def sem(name):
            sems.append(c.enter_context(nc.semaphore("sc_" + name)))
            return sems[-1]

        HI = HD // 2
        NB = WIN // MB
        BLOCKS = T // MB
        PAIRS = MB * (MB - 1) // 2
        R = 4
        NO = NB // 2
        FOLD = 4
        STEPS = 3
        q_, k_, v_, b_ = range(4)
        lanes = sb("lanes", [P, 2, 4, HD, WIN])
        prod, outer = sb("prod", [P, 2, 2, MB, HI, HD + 1]), sb("outer", [P, 2, MB, HI, HD])
        diff = sb("diff", [P, 2, MB, HI])
        xprod = sb("xprod", [P, 2, MB, HI, MB])
        U = sb("U", [P, R, MB, HD])
        X = sb("X", [P, 2, HD, NB, MB * MB])
        ss, inv = sb("ss", [P, WIN]), sb("inv", [P, WIN])
        gprod, G = sb("gprod", [P, PAIRS, HD, NB]), sb("G", [P, PAIRS, NB])
        hprod = sb("hprod", [P, PAIRS + MB, HD, NB])
        sq = hprod[:, 0:MB].rearrange("p c j n -> p (c j n)").rearrange("p (j t) -> p j t", j=HD)
        KQ = sb("KQ", [P, 2, NB, MB * MB])
        N2, T2 = sb("N2", [P, HD, NB, 2]), sb("T2", [P, HD, NB, 2])
        N3, T3 = sb("N3", [P, HD, NB]), sb("T3", [P, HD, NB])
        Sc = sb("Sc", [P, R, HD, HD])
        sqp = sb("sqp", [P, R, MB, HD, HD])
        uq = sb("uq", [P, R, MB, MB, HD])
        ow = sb("ow", [P, 2, HD, WIN])
        zero = sb("zero", [P, HI * HD])
        S = [pb(f"S{h}", [P, 512]) for h in range(2)]
        O = [pb(f"O{h}", [P, 512]) for h in range(2)]
        Gp, Hp = pb("Gp", [P, PAIRS, NB]), pb("Hp", [P, PAIRS + MB, NB])
        (step0, step1, outer_ready0, outer_ready1, S_ready, Sc_ready, u_ready, sqp_ready, o_in_ready, o_ready, ow_ready,
         sq_ready, ss_ready, norm_ready, k_ready, pairs_ready, Gp_ready, Hp_ready, G_ready, chain, x_ready, KQ_ready,
         beta_ready, v_ready, consts) = map(sem, (
                       "step0 step1 outer0 outer1 S_ready Sc_ready u_ready sqp_ready o_in_ready o_ready ow_ready "
                       "sq_ready ss_ready norm_ready k_ready pairs_ready Gp_ready Hp_ready G_ready chain x_ready KQ_ready "
                       "beta_ready v_ready consts").split())
        step = [step0, step1]
        outer_ready = [outer_ready0, outer_ready1]
        loaded, stored = [sem("loaded0"), sem("loaded1")], [sem("out0"), sem("out1")]
        prime(nc, sems)
        block = c.enter_context(nc.Block())
        CH = 13
        BEGIN = 2
        SQUARES = 4
        NORMS = 4
        NORMALIZE = 5
        PAIRS_AT = 5
        PAIR_GROUPS = ((0,), (1, 2), (3,), (4,), (5, 6))
        G_AT, H_AT = 8, 11
        G_PARTS, H_PARTS = 3, NB - H_AT
        G_COPY = 11
        SOLVE = 12

        def lag_of(ap, lag):
            return ap[..., lag * MB:MB * MB:MB + 1]

        def first_pair(lag, with_zero):
            lags = range(0 if with_zero else 1, lag)
            return sum(MB - x for x in lags)

        def steps(s, kind, lo, hi):
            return lanes[:, s, kind].rearrange("p j (n a) -> p j n a", a=MB)[:, :, :, lo:hi]

        @block.sync
        def _(sp):
            def load(w, s):
                sp.dma_start(lanes[:, s].rearrange("p a j t -> p (a j) t"),
                             lanes_dram.rearrange("b (h r) t -> (b h) r t", h=NH)[:, :, bass.ds(w * WIN, WIN)]
                             ).then_inc(loaded[s], 16)

            def store(w, s):
                sp.wait_ge(ow_ready, w * NO + (NO + 1))
                sp.dma_start(scan_dram.rearrange("b (h i) t -> (b h) i t", i=HD)[:, :, bass.ds(w * WIN, WIN)],
                             ow[:, s]).then_inc(stored[s], 16)

            load(0, 0)
            sp.wait_ge(loaded[0], 16 + 1)
            load(1, 1)
            with sp.Fori(0, NWIN // 2 - 1) as p:
                for s in range(2):
                    w = p * 2 + s
                    sp.wait_ge(outer_ready[1], w * NB + (NB + 1))
                    sp.wait_ge(o_in_ready, w * NB + (NB + 1))
                    load(w + 2, s)
                    store(w, s)
            for s in range(2):
                store(NWIN - 2 + s, s)
            for s in range(2):
                sp.wait_ge(stored[s], 16 * (NWIN // 2) + 1)

        @block.scalar
        def _(act):
            def begin(w, s, p):
                act.wait_ge(loaded[s], p * 16 + 17)
                act.wait_ge(ss_ready, w + 1)
                act.activation(lanes[:, s, b_], lanes[:, s, b_], ACT.Sigmoid).then_inc(beta_ready, 1)
                act.activation(sq, lanes[:, s, k_], ACT.Square).then_inc(sq_ready, 1)

            def norms(w):
                act.wait_ge(ss_ready, w + 2)
                act.activation(inv[:], ss[:], ACT.Sqrt).then_inc(norm_ready, 1)

            def copy_g(w, s):
                act.copy(lag_of(X[:, s], 0), steps(s, b_, 0, MB)).then_inc(G_ready, 1)
                act.wait_ge(Gp_ready, w + 2)
                act.activation(G[:], Gp[:], ACT.Copy, scale=-1.0).then_inc(G_ready, 1)

            def copy_h(w, s):
                act.wait_ge(Hp_ready, w + 2)
                for lag in range(MB):
                    at = first_pair(lag, True)
                    act.copy(lag_of(KQ[:, s], lag), Hp[:, at:at + MB - lag, :].rearrange("p c n -> p n c")
                             ).then_inc(KQ_ready, 1)

            def copy_state(n, i):
                for h in range(2):
                    act.wait_ge(step[h], n * STEPS + 2)
                    if later(n, R):
                        act.wait_ge(o_in_ready, n - R + 2)
                    act.copy(Sc[:, i % R, h * HI:(h + 1) * HI, :].rearrange("p i j -> p (i j)"),
                             S[h][:, 0:HI * HD]).then_inc(Sc_ready, 1)

            def put_v(s, i):
                act.activation(prod[:, i % 2, :, :, :, HD], lanes[:, s, v_, :, i * MB:(i + 1) * MB]
                               .rearrange("p (h i) t -> p h t i", h=2), ACT.Copy, scale=-1.0).then_inc(v_ready, 1)

            def evacuate(s, i, n, p):
                so, io = (s, i) if i >= 0 else (1 - s, i + NO)
                act.wait_ge(o_ready, n + 2)
                if i == 0:
                    act.wait_ge(stored[s], p * 16 + 1)
                act.copy(ow[:, so, :, io * 2 * MB:(io + 1) * 2 * MB].rearrange("p i t -> p t i"),
                         O[io % 2][:, 0:2 * MB * HD].rearrange("p (t i) -> p t i", i=HD)).then_inc(ow_ready, 1)

            def window(w, s, p, last=False):
                for i in range(NB):
                    n = w * NB + i
                    copy_state(n, i)
                    if i < NB - 1:
                        put_v(s, i + 1)
                    elif not last:
                        put_v(1 - s, 0)
                    if i == 0:
                        copy_h(w, s)
                    if i % 2 == 0 and later(n, 4):
                        evacuate(s, i // 2 - 2, w * NO + (i // 2 - 2), p)
                    if i == BEGIN and not last:
                        begin(w + 1, 1 - s, p + s)
                    if i == NORMS and not last:
                        norms(w + 1)
                    if i == G_COPY and not last:
                        copy_g(w + 1, 1 - s)

            act.wait_ge(consts, 2)
            begin(0, 0, 0)
            norms(0)
            put_v(0, 0)
            copy_g(0, 0)
            window(0, 0, 0)
            window(1, 1, 0)
            with act.Fori(1, NWIN // 2 - 1) as p:
                for s in range(2):
                    window(p * 2 + s, s, p)
            window(NWIN - 2, 0, NWIN // 2 - 1)
            window(NWIN - 1, 1, NWIN // 2 - 1, last=True)
            for i in range(NO - 2, NO):
                evacuate(1, i, (NWIN - 1) * NO + i, NWIN // 2 - 1)

        @block.tensor
        def _(pe):
            def update(n, slot):
                for h in range(2):
                    pe.wait_ge(outer_ready[h], n + 2)
                    pe.wait_ge(Sc_ready, n * 2 + (h + 2))
                    for t in range(MB):
                        last = pe.matmul(S[h][:, 0:HI * HD], m["ident"][:], outer[:, h, t].rearrange("p i j -> p (i j)"),
                                         start=False, stop=t == MB - 1, skip_group_check=True)
                    last.then_inc(S_ready, 1)

            def outputs(pair, slot, part):
                def product(j):
                    pe.matmul(O[slot // 2][:, 0:2 * MB * HD], m["ident"][:],
                              sqp[:, slot:slot + 2].rearrange("p r t i j -> p (r t i) j")[:, :, j],
                              start=j == 0, stop=False)

                if part == 0:
                    pe.wait_ge(sqp_ready, pair * 2 + 3)
                    if later(pair, 2):
                        pe.wait_ge(ow_ready, pair)
                    for j in range(HD // 2):
                        product(j)
                else:
                    pe.wait_ge(o_in_ready, pair * 2 + 3)
                    for j in range(HD // 2, HD - FOLD):
                        product(j)
                    for x in range(MB):
                        last = pe.matmul(O[slot // 2][:, 0:2 * MB * HD], m["ident"][:], uq[:, slot:slot + 2, :, x, :],
                                         start=False, stop=x == MB - 1)
                    last.then_inc(o_ready, 1)

            def sum_g(w, lo, hi):
                pe.wait_ge(pairs_ready, w * 2 + 2)
                pe.wait_ge(G_ready, w * 2 + 1)
                for j in range(lo, hi):
                    last = pe.matmul(Gp[:], m["ident"][:], gprod[:, :, j, :], start=j == 0, stop=j == HD - 1)
                if hi == HD:
                    last.then_inc(Gp_ready, 1)

            def sum_h(w, lo, hi):
                pe.wait_ge(pairs_ready, w * 2 + 3)
                pe.wait_ge(KQ_ready, w * MB + 1)
                for j in range(lo, hi):
                    last = pe.matmul(Hp[:], m["ident"][:], hprod[:, :, j, :], start=j == 0, stop=j == HD - 1)
                if hi == HD:
                    last.then_inc(Hp_ready, 1)

            def window(w, last=False):
                for b in range(NB):
                    n = w * NB + b
                    update(n, b % R)
                    if later(n, 2):
                        outputs(w * NO + (b // 2 - 1), (b // 2 * 2 - 2) % R, b % 2)
                    if not last:
                        if 0 <= b - G_AT < G_PARTS:
                            sum_g(w + 1, (b - G_AT) * HD // G_PARTS, (b - G_AT + 1) * HD // G_PARTS)
                        if 0 <= b - H_AT < H_PARTS:
                            sum_h(w + 1, (b - H_AT) * HD // H_PARTS, (b - H_AT + 1) * HD // H_PARTS)

            pe.wait_ge(consts, 3)
            for h in range(2):
                pe.matmul(S[h][:, 0:HI * HD], m["ident"][:], zero[:], start=True, stop=True).then_inc(S_ready, 1)
            sum_g(0, 0, HD)
            sum_h(0, 0, HD)
            window(0)
            with pe.Fori(1, NWIN - 1) as w:
                window(w)
            window(NWIN - 1, last=True)
            for part in range(2):
                outputs(BLOCKS // 2 - 1, (BLOCKS - 2) % R, part)

        @block.gpsimd
        def _(pool):
            pool.memset(zero[:], 0.0).then_inc(consts, 1)
            pool.memset(KQ[:], 0.0).then_inc(consts, 1)
            pool.wait_ge(consts, 3)

            def pairs(w, s, k):
                if k == 0:
                    pool.wait_ge(k_ready, w + 2)
                    pool.wait_ge(Gp_ready, w + 1)
                if k == MB - 1:
                    pool.wait_ge(Hp_ready, w + 1)
                keys = k < MB - 1
                lag = k + 1 if keys else k - (MB - 1)
                at = first_pair(lag, not keys)
                last = pool.tensor_tensor((gprod if keys else hprod)[:, at:at + MB - lag].rearrange("p c j n -> p j n c"),
                                          steps(s, k_ if keys else q_, lag, MB), steps(s, k_, 0, MB - lag), ALU.mult)
                if k in (MB - 2, 2 * MB - 2):
                    last.then_inc(pairs_ready, 1)

            def window(w, s, last=False):
                for b in range(NB):
                    n = w * NB + b
                    r = b % R
                    pool.wait_ge(Sc_ready, n * 2 + 3)
                    if later(n, R):
                        pool.wait_ge(o_ready, w * NO + (b // 2 - R // 2 + 2))
                    pool.tensor_tensor(sqp[:, r], mid(Sc[:, r].rearrange("p i j -> p (i j)"), MB)
                                       .rearrange("p t (i j) -> p t i j", j=HD),
                                       lanes[:, s, q_, :, b * MB:(b + 1) * MB].rearrange("p j (t o) -> p t o j", o=1)
                                       .broadcast_to([P, MB, HD, HD]), ALU.mult).then_inc(sqp_ready, 1)
                    pool.wait_ge(sqp_ready, n + 2)
                    kept = sqp[:, r, :, :, HD - 2 * FOLD:HD - FOLD]
                    pool.tensor_tensor(kept, kept, sqp[:, r, :, :, HD - FOLD:HD], ALU.add)
                    pool.wait_ge(u_ready, n * 2 + 3)
                    if b == 0:
                        pool.wait_ge(KQ_ready, w * MB + (MB + 1))
                    pool.tensor_tensor(uq[:, r],
                                       mid(U[:, r].rearrange("p s i -> p (s i)"), MB)
                                       .rearrange("p t (s i) -> p t s i", s=MB),
                                       KQ[:, s, b].rearrange("p (t s o) -> p t s o", t=MB, o=1)
                                       .broadcast_to([P, MB, MB, HD]), ALU.mult).then_inc(o_in_ready, 1)
                    if not last and 0 <= b - PAIRS_AT < len(PAIR_GROUPS):
                        for k in PAIR_GROUPS[b - PAIRS_AT]:
                            pairs(w + 1, 1 - s, k)

            for k in range(2 * MB - 1):
                pairs(0, 0, k)
            window(0, 0)
            window(1, 1)
            with pool.Fori(1, NWIN // 2 - 1) as p:
                for s in range(2):
                    window(p * 2 + s, s)
            window(NWIN - 2, 0)
            window(NWIN - 1, 1, last=True)

        @block.vector
        def _(v):
            def squares(w):
                v.wait_ge(sq_ready, w + 2)
                v.tensor_reduce(ss[:], sq.rearrange("p j t -> p t j"), AX.X, ALU.add).then_inc(ss_ready, 1)

            def normalize(w, s, k):
                if k == 0:
                    v.wait_ge(norm_ready, w + 2)
                    v.tensor_scalar(inv[:], inv[:], NORM_EPS, None, ALU.max).then_inc(chain, 1)
                if k == 1:
                    v.wait_ge(chain, w * CH + 2)
                    v.reciprocal(inv[:], inv[:]).then_inc(chain, 1)
                if k == 2:
                    v.wait_ge(chain, w * CH + 3)
                    v.tensor_tensor(lanes[:, s, k_], lanes[:, s, k_], mid(inv[:], HD), ALU.mult).then_inc(k_ready, 1)

            def solve(w, s, k):
                def g(lag):
                    at = first_pair(lag, False)
                    return G[:, at:at + MB - lag, :].rearrange("p c n -> p n c").rearrange("p n (o c) -> p o n c", o=1) \
                        .broadcast_to([P, HD, NB, MB - lag])

                one = lambda ap: ap.rearrange("p i (n o) -> p i n o", o=1)
                x = lambda a, b: X[:, s, :, :, a * MB + b:a * MB + b + 1]
                if k == 0:
                    v.wait_ge(G_ready, w * 2 + 3)
                    v.wait_ge(beta_ready, w + 2)
                    v.tensor_tensor(lag_of(X[:, s], 1), steps(s, b_, 1, MB), g(1), ALU.mult).then_inc(chain, 1)
                if k == 1:
                    v.wait_ge(chain, w * CH + 4)
                    v.tensor_tensor(N2[:], steps(s, b_, 2, MB), g(2), ALU.mult).then_inc(chain, 1)
                if k == 2:
                    v.wait_ge(chain, w * CH + 5)
                    v.tensor_tensor(one(N3[:]), steps(s, b_, 3, MB), g(3), ALU.mult).then_inc(chain, 1)
                if k == 3:
                    v.wait_ge(chain, w * CH + 6)
                    v.tensor_tensor(T2[:], lag_of(X[:, s], 1)[..., 1:3], lag_of(X[:, s], 1)[..., 0:2], ALU.mult
                                    ).then_inc(chain, 1)
                if k == 4:
                    v.wait_ge(chain, w * CH + 7)
                    v.tensor_tensor(lag_of(X[:, s], 2), N2[:], T2[:], ALU.add).then_inc(chain, 1)
                if k == 5:
                    v.wait_ge(chain, w * CH + 8)
                    v.tensor_tensor(one(T3[:]), N2[:, :, :, 1:2], x(1, 0), ALU.mult).then_inc(chain, 1)
                if k == 6:
                    v.wait_ge(chain, w * CH + 9)
                    v.tensor_tensor(N3[:], N3[:], T3[:], ALU.add).then_inc(chain, 1)
                if k == 7:
                    v.wait_ge(chain, w * CH + 10)
                    v.tensor_tensor(one(T3[:]), x(3, 2), x(2, 0), ALU.mult).then_inc(chain, 1)
                if k == 8:
                    v.wait_ge(chain, w * CH + 11)
                    v.tensor_tensor(x(3, 0), one(N3[:]), one(T3[:]), ALU.add).then_inc(chain, 1)
                for lag in range(1, MB):
                    if k == 8 + lag:
                        v.wait_ge(chain, w * CH + (11 + lag))
                        v.tensor_tensor(lag_of(X[:, s], lag), lag_of(X[:, s], lag), steps(s, b_, 0, MB - lag), ALU.mult
                                        ).then_inc(x_ready if lag == MB - 1 else chain, 1)

            def prepare(w, s, b, k):
                if b == SQUARES and k == 2:
                    squares(w)
                if b == NORMALIZE:
                    normalize(w, s, k)
                if SOLVE <= b < SOLVE + MB:
                    solve(w, s, (b - SOLVE) * 3 + k)

            def window(w, s, last=False):
                for b in range(NB):
                    n = w * NB + b
                    at = slice(b * MB, (b + 1) * MB)
                    key = lanes[:, s, k_, :, at].rearrange("p j (t o) -> p t o j", o=1).broadcast_to([P, MB, HI, HD])
                    half = [slice(h * HI, (h + 1) * HI) for h in range(2)]

                    def free(k):
                        if not last:
                            prepare(w + 1, 1 - s, b, k)

                    def retrieve(h):
                        v.wait_ge(S_ready, n * 2 + (h + 2))
                        v.tensor_tensor(prod[:, b % 2, h, :, :, 0:HD],
                                        mid(S[h][:, 0:HI * HD], MB).rearrange("p t (i j) -> p t i j", j=HD),
                                        key, ALU.mult).then_inc(step[h], 1)

                    def reduce(h, at):
                        v.wait_ge(step[h], at)
                        if h == 0:
                            v.wait_ge(v_ready, n + 2)
                        v.tensor_reduce(diff[:, h], prod[:, b % 2, h], AX.X, ALU.add, negate=True).then_inc(step[h], 1)

                    def apply_x(h, at):
                        v.wait_ge(step[h], at)
                        if b == 0 and h == 0:
                            v.wait_ge(x_ready, w + (MB + 1))
                        v.tensor_tensor(xprod[:, h],
                                        X[:, s, half[h], b, :].rearrange("p i (a b) -> p a i b", b=MB),
                                        mid(diff[:, h].rearrange("p b i -> p (b i)"), MB)
                                        .rearrange("p a (b i) -> p a i b", b=MB),
                                        ALU.mult).then_inc(step[h], 1)

                    def sum_x(h, at):
                        v.wait_ge(step[h], at)
                        if h == 0 and later(n, R):
                            v.wait_ge(o_in_ready, n - R + 2)
                        v.tensor_reduce(U[:, b % R, :, half[h]], xprod[:, h], AX.X, ALU.add).then_inc(u_ready, 1)

                    def expand(h):
                        v.wait_ge(u_ready, n * 2 + (h + 2))
                        v.tensor_tensor(outer[:, h], U[:, b % R, :, half[h]].rearrange("p t (i o) -> p t i o", o=1)
                                        .broadcast_to([P, MB, HI, HD]), key, ALU.mult).then_inc(outer_ready[h], 1)

                    at = n * STEPS
                    retrieve(0)
                    free(0)
                    reduce(0, at + 2)
                    retrieve(1)
                    apply_x(0, at + 3)
                    reduce(1, at + 2)
                    sum_x(0, at + 4)
                    free(1)
                    expand(0)
                    apply_x(1, at + 3)
                    sum_x(1, at + 4)
                    expand(1)
                    free(2)

            for a in range(MB - 1):
                v.memset(X[..., a * MB + a + 1:(a + 1) * MB], 0.0).then_inc(x_ready, 1)
            squares(0)
            for k in range(3):
                normalize(0, 0, k)
            for k in range(3 * MB):
                solve(0, 0, k)
            window(0, 0)
            window(1, 1)
            with v.Fori(1, NWIN // 2 - 1) as p:
                for s in range(2):
                    window(p * 2 + s, s)
            window(NWIN - 2, 0)
            window(NWIN - 1, 1, last=True)


def attn_out(nc, m, scan_dram, w_out, b_out):
    with ExitStack() as c:
        def sb(name, shape, dt=F32):
            return c.enter_context(nc.sbuf_tensor("ao_" + name, shape, dt))

        sems = []

        def sem(name):
            sems.append(c.enter_context(nc.semaphore("ao_" + name)))
            return sems[-1]

        W, bias = sb("w_out_sb", [P, KC, D]), sb("bias", [P, D])
        oT, eps = sb("oT", [P, 2, KC, GN]), sb("eps", [P, 1])
        ps = [c.enter_context(nc.psum_tensor(f"ao_ps{k}", [P, 512], F32)) for k in range(4)]
        w_in, x_scaled, x_biased, y_ready, bank_free, stat, chain, need_sqrt, have_sqrt, eps_ready = map(sem, (
            "w_in", "x_scaled", "x_biased", "y_ready", "bank_free", "stat", "chain", "need_sqrt", "have_sqrt",
            "eps_ready"))
        o_in = [sem("o_in0"), sem("o_in1")]
        prime(nc, sems)
        block = c.enter_context(nc.Block())

        @block.sync
        def _(sp):
            sp.dma_start(W[:], w_out.rearrange("(k p) f -> p k f", p=P)).then_inc(w_in, 16)
            sp.dma_start(bias[:], b_out.rearrange("(o f) -> o f", o=1).broadcast_to([P, D])).then_inc(w_in, 16)

            def load(b, s):
                sp.dma_start(oT[:, s], scan_dram[bass.ds(b, 1), :, s * GN:(s + 1) * GN]
                             .rearrange("o (c p) t -> p (o c) t", p=P)).then_inc(o_in[s], 16)

            for s in range(2):
                load(0, s)
            with sp.Fori(0, B - 1) as b:
                for s in range(2):
                    sp.wait_ge(y_ready, b * 8 + 4 * (s + 1) + 1)
                    load(b + 1, s)

        @block.tensor
        def _(pe):
            pe.wait_ge(w_in, 33)
            with pe.Fori(0, B) as b:
                for s in range(2):
                    pe.wait_ge(o_in[s], b * 16 + 16 + 1)
                    for r in range(GT):
                        pe.wait_ge(bank_free, b * 8 + (4 * s + r + 1) + 1)
                        for k in range(KC):
                            last = pe.matmul(ps[r][:, 0:D], oT[:, s, k, r * P:(r + 1) * P], W[:, k, :],
                                             start=k == 0, stop=k == KC - 1)
                        last.then_inc(y_ready, 1)

        @block.gpsimd
        def _(pool):
            pool.wait_ge(w_in, 33)
            with pool.Fori(0, B) as b:
                for r in range(BT):
                    n = b * BT + r
                    xt = m["x"][:, bass.ds(n, 1), :].rearrange("p o d -> p (o d)")
                    pool.wait_ge(x_scaled, n + 1 + 1)
                    pool.tensor_tensor(xt, xt, bias[:], ALU.add).then_inc(x_biased, 1)

        @block.scalar
        def _(act):
            with act.Fori(0, B) as b:
                for r in range(BT):
                    n = b * BT + r
                    xt = m["x"][:, bass.ds(n, 1), :].rearrange("p o d -> p (o d)")
                    act.activation(xt, xt, ACT.Identity, bias=m["shift1"][:, bass.ds(n, 1)],
                                   scale=m["rs1"][:, bass.ds(n, 1)]).then_inc(x_scaled, 1)
            act.wait_ge(eps_ready, 2)
            act.wait_ge(need_sqrt, 2)
            act.activation(m["r1"][:], m["var"][:], ACT.Sqrt, bias=eps[:]).then_inc(have_sqrt, 1)

        @block.vector
        def _(v):
            link = Chain(v, chain)
            v.memset(eps[:], EPS).then_inc(eps_ready, 1)
            v.nop().then_inc(bank_free, GT)

            def tile(n):
                return m["x"][:, bass.ds(n, 1), :].rearrange("p o d -> p (o d)")

            def moments_of(n):
                v.wait_ge(bank_free, n + GT + 1 + 1)
                v.bn_stats(m["stats"][:, bass.ds(n, 1), :].rearrange("p o s -> p (o s)"), tile(n)).then_inc(stat, 1)

            with v.Fori(0, B) as b:
                for r in range(BT):
                    n = b * BT + r
                    xt = tile(n)
                    v.wait_ge(x_biased, n + 1 + 1)
                    v.wait_ge(y_ready, n + 1 + 1)
                    v.tensor_tensor(xt, xt, ps[r % GT][:, 0:D], ALU.add).then_inc(bank_free, 1)
                    if r > 0:
                        moments_of(n - 1)
                moments_of(b * BT + (BT - 1))
            v.wait_ge(stat, TILES + 1)
            row_moments(v, link, m)
            v.nop().then_inc(need_sqrt, 1)
            v.wait_ge(have_sqrt, 2)
            link(v.reciprocal(m["r1"][:], m["r1"][:]))
            link(v.scalar_tensor_tensor(m["shift1"][:], m["mu"][:], -1.0, m["r1"][:], ALU.mult, ALU.mult))


def route(nc, m, router_w, ws_gate_up, ws_down, rows_dram, counts_dram, ends_dram, out):
    with ExitStack() as c:
        def sb(name, shape, dt=F32):
            return c.enter_context(nc.sbuf_tensor("rt_" + name, shape, dt))

        sems = []

        def sem(name):
            sems.append(c.enter_context(nc.semaphore("rt_" + name)))
            return sems[-1]

        RW, RT = sb("router_rows", [E, D]), sb("router_T", [P, KC, E])
        GU, DN = sb("shared_gu", [P, KC, 2 * F]), sb("shared_dn", [FH, 2, D])
        rows, hT = sb("rows", [P, 2, GT, ROW]), sb("hT", [P, 2, KC, GN])
        neg, m8, e8 = sb("neg", [P, GT]), sb("m8", [P, GT, TOPK]), sb("e8", [P, GT, TOPK])
        ex, rep, mask = sb("ex", [P, GT, E]), sb("rep", [P, GT, E]), sb("mask", [P, GT, E], BF16)
        tri, trif = sb("tri", [P, P + 1], BF16), sb("trif", [P, P + 1])
        cnt, tot = sb("cnt", [E, 2, GT, P]), sb("tot", [E, TILES])
        wsum, carrier = sb("wsum", [P, GT]), sb("carrier", [P, 1])
        th, act_in = sb("th", [FH, 2, GN]), sb("act_in", [FH, 2, GN])
        zero, onesE = sb("zero", [P, ROW]), sb("onesE", [E, TILES])
        tp = [c.enter_context(nc.psum_tensor(f"rt_tp{k}", [P, GN], F32)) for k in range(KC)]
        lg = c.enter_context(nc.psum_tensor("rt_lg", [P, GT, P], F32))
        cp = c.enter_context(nc.psum_tensor("rt_cp", [E, 2, 512], F32))
        gu = [c.enter_context(nc.psum_tensor(f"rt_gu{k}", [P, GN], F32)) for k in range(3)]
        names = ("w_in consts h_ready tp_ready hT_ready lg_ready mx ex_ready topk mask_ready cp_ready cnt_ready "
                 "gate_ready up_ready th_ready t_done a_done dn_ready x_done chain tail_sem id0 rt0 group_chain").split()
        q = {n: sem(n) for n in names}
        rows_out, cnt_out, base_out = ([sem(f"{n}{s}") for s in range(2)] for n in ("rows_out", "cnt_out", "base_out"))
        prime(nc, sems)
        block = c.enter_context(nc.Block())
        groups = 2 * B

        @block.sync
        def _(sp):
            sp.dma_start(RW[:], router_w).then_inc(q["w_in"], 16)
            sp.dma_start(GU[:], ws_gate_up.rearrange("(k p) f -> p k f", p=P)).then_inc(q["w_in"], 16)
            sp.dma_start(DN[:], ws_down.rearrange("(k p) f -> p k f", p=FH)).then_inc(q["w_in"], 16)
            sp.wait_ge(q["consts"], 2)
            sp.dma_start(rows_dram[NT:NT + P, :], zero[:]).then_inc(q["tail_sem"], 16)
            sp.dma_start(out[NT:NT + P, :], zero[:, 0:D]).then_inc(q["tail_sem"], 16)
            def store_rows(g, s):
                sp.wait_ge(q["mask_ready"], g + 1 + 1)
                sp.dma_start(rows_dram.rearrange("(n p) f -> p n f", p=P)[:, bass.ds(g * GT, GT), :],
                             rows[:, s]).then_inc(rows_out[s], 16)

            def two_groups(b, last=False):
                for s in range(2):
                    g = b * 2 + s
                    if not (last and s == 1):
                        store_rows(g + 1, 1 - s)
                    sp.wait_ge(q["cnt_ready"], g + 1 + 1)
                    sp.dma_start(counts_dram.rearrange("(e n) t -> e n t", e=E)[:, bass.ds(g * GT, GT), :],
                                 cnt[:, s]).then_inc(cnt_out[s], 16)
                    sp.wait_ge(q["x_done"], g * GT + GT + 1)
                    sp.dma_start(out.rearrange("(n p) f -> p n f", p=P)[:, bass.ds(g * GT, GT), :],
                                 m["x"][:, bass.ds(g * GT, GT), :]).then_inc(base_out[s], 16)

            store_rows(0, 0)
            with sp.Fori(0, B - 1) as b:
                two_groups(b)
            two_groups(B - 1, last=True)
            sp.wait_ge(q["chain"], 2)
            sp.dma_start(ends_dram.rearrange("o (e n) -> (o e) n", e=E), tot[:]).then_inc(q["tail_sem"], 16)
            sp.wait_ge(q["tail_sem"], 49)
            for s in range(2):
                for x in (rows_out, cnt_out, base_out):
                    sp.wait_ge(x[s], 16 * B + 1)

        @block.gpsimd
        def _(pool):
            pool.memset(zero[:], 0.0).then_inc(q["consts"], 1)
            pool.memset(onesE[:], 1.0).then_inc(q["consts"], 1)
            pool.memset(trif[:], 2.0).then_inc(q["id0"], 1)
            pool.wait_ge(q["id0"], 2)
            pool.affine_select(out=trif[:, 0:P], in_=trif[:, 0:P], compare_op=ALU.is_ge, fill=0.0, base=0,
                               pattern=[[1, P]], channel_multiplier=-1).then_inc(q["id0"], 1)
            pool.wait_ge(q["id0"], 3)
            pool.tensor_tensor(trif[:, 0:P], trif[:, 0:P], m["ident"][:], ALU.subtract).then_inc(q["id0"], 1)
            pool.wait_ge(q["id0"], 4)
            pool.tensor_copy(tri[:], trif[:]).then_inc(q["consts"], 1)

        @block.tensor
        def _(pe):
            pe.wait_ge(q["w_in"], 49)
            for k in range(KC):
                last = pe.transpose(tp[k][:, 0:E], RW[:, k * P:(k + 1) * P], m["ident"][0:E, 0:E])
            last.then_inc(q["rt0"], 1)
            pe.wait_ge(q["rt0"], 4)
            pe.wait_ge(q["consts"], 4)

            def transposes(g, s):
                pe.wait_ge(q["hT_ready"], g * 2 + 1)
                pe.wait_ge(q["h_ready"], g * GT + GT + 1)
                for r in range(GT):
                    for k in range(KC):
                        last = pe.transpose(tp[k][:, r * P:(r + 1) * P], rows[:, s, r, k * P:(k + 1) * P],
                                            m["ident"][:])
                last.then_inc(q["tp_ready"], 1)

            def logits(g, s):
                pe.wait_ge(q["hT_ready"], g * 2 + 2 + 1)
                pe.wait_ge(q["ex_ready"], g * GT + 1)
                for r in range(GT):
                    for k in range(KC):
                        last = pe.matmul(lg[:, r, 0:E], hT[:, s, k, r * P:(r + 1) * P], RT[:, k, :],
                                         start=k == 0, stop=k == KC - 1)
                last.then_inc(q["lg_ready"], 1)

            def gate_up(g, s, f):
                pe.wait_ge(q["t_done"], g * 2 + f + 1)
                for j in range(KC):
                    last = pe.matmul(gu[0][0:FH, :], GU[:, j, f * FH:(f + 1) * FH], hT[:, s, j, :],
                                     start=j == 0, stop=j == KC - 1)
                last.then_inc(q["gate_ready"], 1)
                pe.wait_ge(q["a_done"], g * 2 + f + 1)
                if f == 0:
                    pe.wait_ge(q["x_done"], g * GT + 1)
                for j in range(KC):
                    last = pe.matmul(gu[1][0:FH, :], GU[:, j, F + f * FH:F + (f + 1) * FH], hT[:, s, j, :],
                                     start=j == 0, stop=j == KC - 1)
                last.then_inc(q["up_ready"], 1)

            def counts(g):
                pe.wait_ge(q["mask_ready"], g + 1 + 1)
                pe.wait_ge(q["cnt_ready"], g + 1)
                for r in range(GT):
                    last = pe.matmul(cp[:, r // 2, (r % 2) * 256:(r % 2) * 256 + P + 1], mask[:, r, :], tri[:],
                                     start=True, stop=True)
                last.then_inc(q["cp_ready"], 1)

            def down(g):
                pe.wait_ge(q["a_done"], g * 2 + 2 + 1)
                for r in range(GT):
                    if r >= 2:
                        pe.wait_ge(q["x_done"], g * GT + (r - 1) + 1)
                    for f in range(2):
                        last = pe.matmul(gu[2 - r % 2][:, 0:D], act_in[:, f, r * P:(r + 1) * P], DN[:, f, :],
                                         start=f == 0, stop=f == 1)
                    last.then_inc(q["dn_ready"], 1)

            def two_groups(b, last=False):
                for s in range(2):
                    g = b * 2 + s
                    gate_up(g, s, 0)
                    if not (last and s == 1):
                        logits(g + 1, 1 - s)
                    counts(g)
                    gate_up(g, s, 1)
                    if not last:
                        transposes(g + 2, s)
                    down(g)

            transposes(0, 0)
            logits(0, 0)
            transposes(1, 1)
            with pe.Fori(0, B - 1) as b:
                two_groups(b)
            two_groups(B - 1, last=True)

        @block.scalar
        def _(act):
            act.wait_ge(q["rt0"], 2)
            for k in range(KC):
                act.copy(RT[:, k, :], tp[k][:, 0:E]).then_inc(q["rt0"], 1)

            def normalize(b, s):
                for r in range(GT):
                    n = b * BT + (s * GT + r)
                    act.activation(rows[:, s, r, 0:D], m["x"][:, bass.ds(n, 1), :].rearrange("p o d -> p (o d)"),
                                   ACT.Identity, bias=m["shift1"][:, bass.ds(n, 1)], scale=m["r1"][:, bass.ds(n, 1)]
                                   ).then_inc(q["h_ready"], 1)

            def copy_hT(g, s):
                act.wait_ge(q["tp_ready"], g + 1 + 1)
                if later(g, 2):
                    act.wait_ge(q["up_ready"], g * 2 - 1)
                for k in range(KC):
                    act.copy(hT[:, s, k, :], tp[k][:]).then_inc(q["hT_ready"], 1)

            def exponents(g):
                for r in range(GT):
                    act.wait_ge(q["mx"], g * GT + GT + 1)
                    act.activation(ex[:, r, :], lg[:, r, 0:E], ACT.Exp, bias=neg[:, r:r + 1]
                                   ).then_inc(q["ex_ready"], 1)

            def tanh(g, f):
                act.wait_ge(q["gate_ready"], g * 2 + (f + 1) + 1)
                act.wait_ge(q["t_done"], g * 2 + 1)
                act.activation(th[:, f, :], gu[0][0:FH, :], ACT.Tanh, scale=0.5).then_inc(q["th_ready"], 1)

            def two_groups(b, last=False):
                for s in range(2):
                    g = b * 2 + s
                    tanh(g, 0)
                    if not (last and s == 1):
                        exponents(g + 1)
                    act.wait_ge(q["cp_ready"], g + 1 + 1)
                    act.wait_ge(cnt_out[s], b * 16 + 1)
                    act.copy(tot[:, bass.ds(g * GT, GT)].rearrange("e (a r) -> e a r", r=2),
                             cp[:].rearrange("e a (r t) -> e a r t", r=2)[:, :, :, P]).then_inc(q["topk"], 1)
                    act.copy(cnt[:, s].rearrange("e (a r) t -> e a r t", r=2),
                             cp[:].rearrange("e a (r t) -> e a r t", r=2)[:, :, :, 0:P]).then_inc(q["cnt_ready"], 1)
                    if not last:
                        act.wait_ge(rows_out[s], b * 16 + 16 + 1)
                        normalize(b + 1, s)
                    tanh(g, 1)
                    if not last:
                        copy_hT(g + 2, s)

            normalize(0, 0)
            copy_hT(0, 0)
            normalize(0, 1)
            copy_hT(1, 1)
            exponents(0)
            with act.Fori(0, B - 1) as b:
                two_groups(b)
            two_groups(B - 1, last=True)

        @block.vector
        def _(v):
            L = 9

            def maxima(g):
                link = Chain(v, cs, g * L)
                v.wait_ge(q["lg_ready"], g + 1 + 1)
                v.memset(carrier[:], 0.0)
                for r in range(GT):
                    last = v.max(m8[:, r, :], lg[:, r, 0:E])
                link(last)
                v.wait_ge(q["ex_ready"], g * GT + 1)
                link(v.tensor_scalar(neg[:], m8[:, :, 0], -1.0, None, ALU.mult))
                v.nop().then_inc(q["mx"], GT)

            def top_k(g, s):
                link = Chain(v, cs, g * L + 2)
                v.wait_ge(q["ex_ready"], g * GT + GT + 1)
                v.memset(carrier[:], 0.0)
                for r in range(GT):
                    last = v.max(e8[:, r, :], ex[:, r, :])
                link(last)
                link(v.tensor_reduce(wsum[:], e8[:], AX.X, ALU.add))
                link(v.reciprocal(wsum[:], wsum[:]))
                v.memset(carrier[:], 0.0)
                for r in range(GT):
                    last = v.match_replace(rep[:, r, :], e8[:, r, :], ex[:, r, :], -1.0)
                link(last)
                v.wait_ge(q["cp_ready"], g + 1)
                link(v.tensor_scalar(mask[:], rep[:], 0.0, None, ALU.is_lt))
                link(v.tensor_tensor(ex[:], ex[:], mask[:], ALU.mult))
                link(v.tensor_tensor(rows[:, s, :, D:ROW], ex[:],
                                     wsum[:].rearrange("p (r o) -> p r o", o=1).broadcast_to([P, GT, E]), ALU.mult))
                v.nop().then_inc(q["mask_ready"], 1)

            def swish(g, f):
                v.wait_ge(q["th_ready"], g * 2 + (f + 1) + 1)
                v.scalar_tensor_tensor(th[:, f, :], th[:, f, :], 1.0, gu[0][0:FH, :], ALU.add, ALU.mult
                                       ).then_inc(q["t_done"], 1)
                v.wait_ge(q["t_done"], g * 2 + (f + 1) + 1)
                v.wait_ge(q["up_ready"], g * 2 + (f + 1) + 1)
                v.wait_ge(q["dn_ready"], g * GT + 1)
                v.scalar_tensor_tensor(act_in[:, f, :], th[:, f, :], 0.5, gu[1][0:FH, :], ALU.mult, ALU.mult
                                       ).then_inc(q["a_done"], 1)

            def two_groups(b, last=False):
                for s in range(2):
                    g = b * 2 + s
                    swish(g, 0)
                    if not (last and s == 1):
                        maxima(g + 1)
                        top_k(g + 1, 1 - s)
                    swish(g, 1)
                    for r in range(GT):
                        n = b * BT + (s * GT + r)
                        xt = m["x"][:, bass.ds(n, 1), :].rearrange("p o d -> p (o d)")
                        v.wait_ge(q["dn_ready"], n + 1 + 1)
                        v.tensor_tensor(xt, xt, gu[2 - r % 2][:, 0:D], ALU.add).then_inc(q["x_done"], 1)

            cs = q["group_chain"]
            maxima(0)
            top_k(0, 0)
            with v.Fori(0, B - 1) as b:
                two_groups(b)
            two_groups(B - 1, last=True)
            v.wait_ge(q["topk"], groups + 1)
            v.wait_ge(q["consts"], 3)
            v.tensor_scalar(tot[:], tot[:], 0.5, None, ALU.mult).then_inc(cs, 1)
            v.wait_ge(cs, groups * L + 1 + 1)
            v.tensor_tensor_scan(tot[:], onesE[:], tot[:], 0.0, ALU.mult, ALU.add).then_inc(q["chain"], 1)


def experts(nc, w_gate, w_up, w_down, rows_dram, counts_dram, ends_dram, out):
    R = 8
    ITS = E // R
    Z = 3
    CA, CB = 7, 4
    PA = CB + 1
    FIRST = 2 + CB
    with ExitStack() as c:
        def sb(name, shape, dt=F32):
            return c.enter_context(nc.sbuf_tensor("ex_" + name, shape, dt))

        sems = []

        def sem(name):
            sems.append(c.enter_context(nc.semaphore("ex_" + name)))
            return sems[-1]

        ident = sb("ident2", [P, P])
        ends, le = sb("ends", [P, E, TILES]), sb("le", [P, E, TILES])
        carrier, zero = sb("carrier", [P, R + FIRST]), sb("zero", [P, 1])
        slot, tok = sb("slot", [P, 1]), sb("tok", [P, P])
        tile_of, first, none, goal = sb("tile_of", [P, E]), sb("first", [P, E]), sb("none", [P, E]), sb("goal", [P, E])
        row_f, base = sb("row_f", [P, E]), sb("base", [P, E])
        row_id = sb("row_id", [P, E], U32)
        eoff = sb("eoff", [P, E])
        row_cur, tok_cur = sb("row_cur", [P, R], U32), sb("tok_cur", [P, R], U32)
        vr, junk, pos = sb("vr", [P, R, P]), sb("junk", [P, R, P]), sb("pos", [P, R])
        WGU, WD = sb("wgu", [P, R, 2, KC, F]), sb("wd", [FH, R, 2, D])
        xg, xT = sb("xg", [P, R, ROW]), sb("xT", [P, 2, KC, P])
        th, t2, aT, yw = sb("th", [FH, 2, 2, P]), sb("t2", [FH, 2, 2, P]), sb("aT", [FH, 2, 2, P]), sb("yw", [P, R, D])
        tp = [c.enter_context(nc.psum_tensor(f"ex_tp{k}", [P, 512], F32)) for k in range(2)]
        gu = [c.enter_context(nc.psum_tensor(f"ex_gu{k}", [P, 4, P], F32)) for k in range(2)]
        yp = [c.enter_context(nc.psum_tensor(f"ex_yp{k}", [P, 512], F32)) for k in range(2)]
        (ends_in, consts, chain, row_copied, pos_done, tok_ready, tp_ready, xT_ready, gu_ready, th_ready, t2_ready,
         a_ready, y_ready, yw_ready, id0, carried) = map(sem, (
             "ends_in consts chain row_copied pos_done tok_ready tp_ready xT_ready gu_ready th_ready t2_ready "
             "a_ready y_ready yw_ready id0 carried").split())
        prime(nc, sems, Z)
        w_in, v_in, x_in, added = ([sem(f"{n}{s}") for s in range(R)] for n in ("w_in", "v_in", "x_in", "added"))
        block = c.enter_context(nc.Block())

        def ring(it, s, ahead):
            return (s + ahead) % R, it + ((s + ahead) // R + 1)

        def has(e):
            return not isinstance(e, int) or e < E

        @block.sync
        def _(sp):
            def load(e, s):
                for g, w in enumerate((w_gate, w_up)):
                    sp.dma_start(WGU[:, s, g], w[bass.ds(e, 1)].rearrange("o (k p) f -> p (o k) f", p=P)
                                 ).then_inc(w_in[s], 16)
                sp.dma_start(WD[:, s], w_down[bass.ds(e, 1)].rearrange("o (k p) f -> p (o k) f", p=FH)
                             ).then_inc(w_in[s], 16)

            sp.dma_start(ends[:].rearrange("p e n -> p (e n)"), ends_dram.broadcast_to([P, E * TILES])
                         ).then_inc(ends_in, 16)
            for s in range(R):
                load(s, s)
            with sp.Fori(0, ITS - 1) as it:
                for s in range(R):
                    sp.wait_ge(y_ready, it * R + (s + 1 + Z))
                    load(it * R + (s + R), s)

        @block.gpsimd
        def _(pool):
            def carry(k):
                pool.tensor_tensor(carrier[:, k:k + 1], zero[:], zero[:], ALU.add).then_inc(carried, 1)

            def gather_counts(s):
                pool.indirect_dma_start(
                    out=vr[:, s], out_offset=None, in_=counts_dram,
                    in_offset=bass.IndirectOffsetOnAxis(ap=row_cur[:, s:s + 1], axis=0),
                    bounds_check=E * TILES - 1).then_inc(v_in[s], 16)

            def gather_rows(s):
                pool.indirect_dma_start(
                    out=xg[:, s], out_offset=None, in_=rows_dram,
                    in_offset=bass.IndirectOffsetOnAxis(ap=tok_cur[:, s:s + 1], axis=0),
                    bounds_check=NT + P - 1).then_inc(x_in[s], 16)

            def add(s):
                pool.indirect_dma_start(
                    out=out, out_offset=bass.IndirectOffsetOnAxis(ap=tok_cur[:, s:s + 1], axis=0),
                    in_=yw[:, s], in_offset=None, bounds_check=NT + P - 1, compute_op=ALU.add
                ).then_inc(added[s], 16)

            def wait_inputs(e):
                pool.wait_ge(yw_ready, e + (1 + Z))
                if has(e + CA):
                    pool.wait_ge(row_copied, e + (CA + 1 + Z))
                if has(e + CB):
                    pool.wait_ge(tok_ready, e + (CB + 1 + Z))

            def experts_of(it):
                for s in range(R):
                    e = it * R + s
                    add(s)
                    if has(e + CA):
                        gather_counts((s + CA) % R)
                    if has(e + CB):
                        gather_rows((s + CB) % R)
                    pool.wait_ge(added[s], it * 16 + 16)
                    if has(e + 1):
                        wait_inputs(e + 1)
                    carry(s)

            pool.memset(zero[:], 0.0).then_inc(consts, 1)
            pool.wait_ge(consts, 1 + Z)
            pool.memset(ident[:], 0.0).then_inc(id0, 1)
            pool.wait_ge(id0, 1 + Z)
            pool.affine_select(out=ident[:], in_=ident[:], compare_op=ALU.not_equal, fill=1.0,
                               base=0, pattern=[[-1, P]], channel_multiplier=1).then_inc(consts, 1)
            pool.iota(slot[:], pattern=[[0, 1]], base=0, channel_multiplier=1,
                      allow_small_or_imprecise_dtypes=True).then_inc(consts, 1)
            pool.iota(tok[:], pattern=[[1, P]], base=0, channel_multiplier=0,
                      allow_small_or_imprecise_dtypes=True).then_inc(consts, 1)
            pool.iota(eoff[:], pattern=[[TILES, E]], base=0, channel_multiplier=0,
                      allow_small_or_imprecise_dtypes=True).then_inc(consts, 1)
            pool.wait_ge(row_copied, CA + Z)
            carry(R)
            for e in range(CA):
                gather_counts(e)
            for e in range(CB):
                pool.wait_ge(tok_ready, e + 1 + Z)
                carry(R + 1 + e)
                gather_rows(e)
            wait_inputs(0)
            carry(R + 1 + CB)
            with pool.Fori(0, ITS - 1) as it:
                experts_of(it)
            experts_of(ITS - 1)

        @block.tensor
        def _(pe):
            def transposes(e, it, s, ahead):
                r, fills = ring(it, s, ahead)
                d = r % 2
                pe.wait_ge(x_in[r], fills * 16)
                pe.wait_ge(xT_ready, e + (-1 + Z))
                for k in range(KC):
                    last = pe.transpose(tp[d][:, k * P:(k + 1) * P], xg[:, r, k * P:(k + 1) * P], ident[:])
                last.then_inc(tp_ready, 1)

            def gate_up(e, it, s, ahead):
                r, fills = ring(it, s, ahead)
                d = r % 2
                pe.wait_ge(w_in[r], fills * 48)
                pe.wait_ge(xT_ready, e + (1 + Z))
                pe.wait_ge(a_ready, e + (-1 + Z))
                for g in range(2):
                    for f in range(2):
                        for k in range(KC):
                            last = pe.matmul(gu[d][0:FH, g * 2 + f, :], WGU[:, r, g, k, f * FH:(f + 1) * FH],
                                             xT[:, d, k, :], start=k == 0, stop=k == KC - 1)
                last.then_inc(gu_ready, 1)

            def down(e, it, s):
                d = s % 2
                pe.wait_ge(a_ready, e + (1 + Z))
                pe.wait_ge(yw_ready, e + (-1 + Z))
                for f in range(2):
                    last = pe.matmul(yp[d][:, 0:D], aT[:, d, f, :], WD[:, s, f, :], start=f == 0, stop=f == 1)
                last.then_inc(y_ready, 1)

            def experts_of(it):
                for s in range(R):
                    e = it * R + s
                    if has(e + 1):
                        gate_up(e + 1, it, s, 1)
                    if has(e + 2):
                        transposes(e + 2, it, s, 2)
                    down(e, it, s)

            pe.wait_ge(consts, 2 + Z)
            transposes(0, 0, 0, 0)
            gate_up(0, 0, 0, 0)
            transposes(1, 0, 1, 0)
            with pe.Fori(0, ITS - 1) as it:
                experts_of(it)
            experts_of(ITS - 1)

        @block.scalar
        def _(act):
            def copy_xT(e, d):
                act.wait_ge(tp_ready, e + (1 + Z))
                act.wait_ge(gu_ready, e + (-1 + Z))
                act.copy(xT[:, d].rearrange("p k t -> p (k t)"), tp[d][:, 0:KC * P]).then_inc(xT_ready, 1)

            def tanh(e, d):
                act.wait_ge(gu_ready, e + (1 + Z))
                act.wait_ge(t2_ready, e + (-1 + Z))
                act.activation(th[:, d], gu[d][0:FH, 0:2, :], ACT.Tanh, scale=0.5).then_inc(th_ready, 1)

            def experts_of(it):
                for s in range(R):
                    e = it * R + s
                    if has(e + 1):
                        tanh(e + 1, (s + 1) % 2)
                    if has(e + 2):
                        copy_xT(e + 2, s % 2)
                    act.wait_ge(y_ready, e + (1 + Z))
                    act.activation(yw[:, s], yp[s % 2][:, 0:D], ACT.Copy, scale=xg[:, s, bass.ds(e + D, 1)]
                                   ).then_inc(yw_ready, 1)

            copy_xT(0, 0)
            tanh(0, 0)
            copy_xT(1, 1)
            with act.Fori(0, ITS - 1) as it:
                experts_of(it)
            experts_of(ITS - 1)

        @block.vector
        def _(v):
            def copy_row(e, s):
                v.tensor_copy(row_cur[:, s:s + 1], row_id[:, bass.ds(e, 1)]).then_inc(row_copied, 1)

            def token(e, it, s, ahead):
                r, fills = ring(it, s, ahead)
                v.wait_ge(v_in[r], fills * 16)
                v.scalar_tensor_tensor(junk[:, r], vr[:, r], goal[:, bass.ds(e, 1)], tok[:], ALU.is_equal,
                                       ALU.mult, accum_out=pos[:, r:r + 1]).then_inc(pos_done, 1)
                v.wait_ge(pos_done, e + (1 + Z))
                if later(e, R):
                    v.wait_ge(carried, e + (1 - R + FIRST + Z))
                v.tensor_tensor(tok_cur[:, r:r + 1], pos[:, r:r + 1], base[:, bass.ds(e, 1)], ALU.add
                                ).then_inc(tok_ready, 1)

            def experts_of(it):
                for s in range(R):
                    e, d = it * R + s, s % 2
                    if has(e + R):
                        copy_row(e + R, s)
                    v.wait_ge(th_ready, e + (1 + Z))
                    v.scalar_tensor_tensor(t2[:, d], th[:, d], 1.0, gu[d][0:FH, 0:2, :], ALU.add, ALU.mult
                                           ).then_inc(t2_ready, 1)
                    v.wait_ge(t2_ready, e + (1 + Z))
                    v.wait_ge(y_ready, e + (-1 + Z))
                    v.scalar_tensor_tensor(aT[:, d], t2[:, d], 0.5, gu[d][0:FH, 2:4, :], ALU.mult, ALU.mult
                                           ).then_inc(a_ready, 1)
                    if has(e + PA):
                        token(e + PA, it, s, PA)

            link = Chain(v, chain, first=Z)
            v.wait_ge(ends_in, 16 + Z)
            v.wait_ge(consts, 5 + Z)
            sc = slot[:, 0:1]
            link(v.tensor_scalar(le[:], ends[:], sc, None, ALU.is_le))
            link(v.tensor_reduce(tile_of[:], le[:], AX.X, ALU.add))
            link(v.tensor_scalar(row_f[:], tile_of[:], float(TILES - 1), None, ALU.min))
            link(v.tensor_tensor(row_f[:], row_f[:], eoff[:], ALU.add))
            link(v.tensor_copy(row_id[:], row_f[:]))
            for e in range(R):
                copy_row(e, e)
            link(v.tensor_tensor(le[:], le[:], ends[:], ALU.mult))
            link(v.tensor_reduce(first[:], le[:], AX.X, ALU.max))
            link(v.tensor_scalar(none[:], tile_of[:], float(TILES), None, ALU.is_ge))
            link(v.tensor_scalar(goal[:], first[:], sc, -2.0, ALU.subtract, ALU.mult))
            link(v.tensor_scalar(goal[:], goal[:], 1.0, None, ALU.add))
            link(v.scalar_tensor_tensor(goal[:], none[:], -4.0 * NT, goal[:], ALU.mult, ALU.add))
            link(v.tensor_scalar(base[:], none[:], sc, None, ALU.mult))
            link(v.scalar_tensor_tensor(base[:], tile_of[:], float(P), base[:], ALU.mult, ALU.add))
            for e in range(PA):
                token(e, 0, e, 0)
            with v.Fori(0, ITS - 1) as it:
                experts_of(it)
            experts_of(ITS - 1)


_INS = ['L0_attn_x', 'L0_attn_ln_g', 'L0_attn_ln_b', 'L0_attn_w_qkvb', 'L0_attn_b_qkvb', 'L0_attn_w_out',
        'L0_attn_b_out', 'L0_ffn_router_w', 'L0_ffn_w_gate', 'L0_ffn_w_up', 'L0_ffn_w_down',
        'L0_ffn_ws_gate_up', 'L0_ffn_ws_down']


def kernel(**inputs):
    import numpy as _np
    import concourse.bacc as _bacc
    from concourse import mybir as _mybir
    from concourse.bass_utils import run_bass_kernel_spmd as _run

    nc = _bacc.Bacc("TRN2", target_bir_lowering=False, num_devices=1)
    arrays, args = {}, []
    for name in _INS:
        a = _np.ascontiguousarray(inputs[name])
        arrays[f"in_{name}_dram"] = a
        args.append(nc.dram_tensor(f"in_{name}_dram", a.shape, _mybir.dt.from_np(a.dtype), kind="ExternalInput").ap())
    args.append(nc.dram_tensor("out_0_dram", (NT + P, D), F32, kind="ExternalOutput").ap())
    build(nc, *args)
    r = _run(nc, [arrays], core_ids=[0])
    return r.results[0]["out_0_dram"][0:NT].reshape(B, T, D)
```
